# Optimizing a Trainium2 kernel written in Bass

```python
import numpy as np
import jax
import jax.numpy as jnp

def _softmax(x, axis=-1):
    return jax.nn.softmax(x, axis=axis)

def _gelu(x):
    return jax.nn.gelu(x, approximate=True)

def _silu(x):
    return jax.nn.silu(x)

def _sigmoid(x):
    return jax.nn.sigmoid(x)

def _layernorm(x, axis=-1, eps=1e-05):
    m = jnp.mean(x, axis=axis, keepdims=True)
    v = jnp.var(x, axis=axis, keepdims=True)
    return (x - m) / jnp.sqrt(v + eps)

def _scatter_add(tgt, idx, src, axis=0):
    return tgt.at[idx].add(src)

def _segment_sum(src, seg, n):
    return jax.ops.segment_sum(src, seg, n)
kernel_name = 'mk_decoder_postln_d1_seqx_r8_706f54'

def setup_inputs(seed: int=0):
    np.random.seed(seed)
    _w = jnp.asarray

    def _rec_inputs():
        import jax
        import jax.numpy as jnp
        _rk = jax.random.key(seed)
        x = 7.22e-05 + 1 * jax.random.normal(jax.random.fold_in(_rk, 1), (4, 512, 128), jnp.float32)
        _lenS = 512 - jax.random.randint(jax.random.fold_in(_rk, 7), (4,), 0, max(1, 512 // 4) + 1, jnp.int32)
        _lenS2 = 77 - jax.random.randint(jax.random.fold_in(_rk, 8), (4,), 0, max(1, 77 // 4) + 1, jnp.int32)
        _ctx_1024P = jax.random.normal(jax.random.fold_in(_rk, 11), (4, 16, 128), jnp.float32)
        _ctx_1024c = jax.random.dirichlet(jax.random.fold_in(_rk, 511), 0.3 * jnp.ones((16,), jnp.float32), (4, 77))
        _ctx_1024t = jnp.einsum('bsk,bkd->bsd', _ctx_1024c, _ctx_1024P)
        _ctx_1024t = _ctx_1024t * jax.lax.rsqrt(jnp.mean(jnp.square(_ctx_1024t)) + 1e-12) * 0.953939
        ctx_1024 = 4.13588e-05 + 0.999923 * (_ctx_1024t + 0.3 * jax.random.normal(jax.random.fold_in(_rk, 611), (4, 77, 128), jnp.float32))
        return (x, ctx_1024)
    x, ctx_1024 = _rec_inputs()

    def _L0_attn_setup():
        import jax, jax.numpy as jnp
        from jax import lax
        import numpy as np
        D_MODEL = 128
        D_STATE = 64
        D_CONV = 4
        EXPAND = 2
        HEADDIM = 128
        NGROUPS = 1
        CHUNK = 32
        D_INNER = EXPAND * D_MODEL
        NHEADS = D_INNER // HEADDIM
        CONV_DIM = D_INNER + 2 * NGROUPS * D_STATE
        D_IN_PROJ = D_INNER + CONV_DIM + NHEADS

        def _segsum_exp(t):
            T = t.shape[-1]
            cs = jnp.cumsum(t, axis=-1)
            d = cs[..., :, None] - cs[..., None, :]
            mask = jnp.tril(jnp.ones((T, T), dtype=bool))
            return jnp.where(mask, jnp.exp(jnp.where(mask, d, 0.0)), 0.0)

        def _ssd_scan(x, dt, A, Bm, Cm, chunk):
            Bz, L, H, P = x.shape
            G, N = (Bm.shape[2], Bm.shape[3])
            nc = L // chunk
            rep = H // G
            Bh = jnp.repeat(Bm, rep, axis=2)
            Ch = jnp.repeat(Cm, rep, axis=2)
            xc = x.reshape(Bz, nc, chunk, H, P)
            dtc = dt.reshape(Bz, nc, chunk, H)
            Bc = Bh.reshape(Bz, nc, chunk, H, N)
            Cc = Ch.reshape(Bz, nc, chunk, H, N)
            dA = dtc * A[None, None, None, :]
            dAh = jnp.transpose(dA, (0, 1, 3, 2))
            A_cs = jnp.cumsum(dAh, axis=-1)
            Lmat = _segsum_exp(dAh)
            Y_diag = jnp.einsum('bcqhn,bckhn,bchqk,bckh,bckhp->bcqhp', Cc, Bc, Lmat, dtc, xc)
            decay_states = jnp.exp(A_cs[..., -1:] - A_cs)
            states = jnp.einsum('bckhn,bchk,bckh,bckhp->bchpn', Bc, decay_states, dtc, xc)
            chunk_total = jnp.transpose(A_cs[..., -1], (0, 2, 1))
            padded = jnp.pad(chunk_total, ((0, 0), (0, 0), (1, 0)))
            decay_chunk = _segsum_exp(padded)
            states_cat = jnp.concatenate([jnp.zeros_like(states[:, :1]), states], axis=1)
            new_states = jnp.einsum('bhzc,bchpn->bzhpn', decay_chunk, states_cat)
            prev = new_states[:, :-1]
            Y_off = jnp.einsum('bcqhn,bchpn,bchq->bcqhp', Cc, prev, jnp.exp(A_cs))
            return (Y_diag + Y_off).reshape(Bz, L, H, P)
        key = jax.random.key(seed)
        ks = jax.random.split(key, 8)
        x = jax.random.normal(ks[0], (2, 512, D_MODEL), dtype=jnp.float32)
        W_in = jax.random.normal(ks[1], (D_IN_PROJ, D_MODEL), dtype=jnp.float32) * 0.02
        conv_w = jax.random.normal(ks[2], (CONV_DIM, 1, D_CONV), dtype=jnp.float32) * 0.2
        conv_b = jnp.zeros((CONV_DIM,), dtype=jnp.float32)
        A_init = jax.random.uniform(ks[3], (NHEADS,), minval=1.0, maxval=16.0)
        A_log = jnp.log(A_init).astype(jnp.float32)
        dtv = jnp.exp(jax.random.uniform(ks[4], (NHEADS,)) * (np.log(0.1) - np.log(0.001)) + np.log(0.001))
        dtv = jnp.clip(dtv, 0.001, None)
        dt_bias = (dtv + jnp.log(-jnp.expm1(-dtv))).astype(jnp.float32)
        D_skip = jnp.ones((NHEADS,), dtype=jnp.float32)
        W_out = jax.random.normal(ks[5], (D_MODEL, D_INNER), dtype=jnp.float32) * 0.02
        return {'x': x, 'W_in': W_in, 'conv_w': conv_w, 'conv_b': conv_b, 'A_log': A_log, 'dt_bias': dt_bias, 'D_skip': D_skip, 'W_out': W_out}
    _L0_attn_all = _L0_attn_setup()
    _L0_attn_in = {k: v for k, v in _L0_attn_all.items() if k in ('W_in', 'conv_w', 'conv_b', 'A_log', 'dt_bias', 'D_skip', 'W_out')}
    del _L0_attn_all

    def _L0_xattn_setup():
        import jax, jax.numpy as jnp
        import numpy as np
        EMBED = 128
        HEADS = 16
        HEAD_DIM = EMBED // HEADS
        key = jax.random.key(seed)
        ks = jax.random.split(key, 12)
        B, S, D = (4, 256, EMBED)
        scale = 1.0 / np.sqrt(D)
        inp = {'query': jax.random.normal(ks[0], (B, S, D), dtype=jnp.float32), 'key': jax.random.normal(ks[1], (B, S, D), dtype=jnp.float32), 'value': jax.random.normal(ks[2], (B, S, D), dtype=jnp.float32), 'Wq': jax.random.normal(ks[3], (D, D), dtype=jnp.float32) * scale, 'bq': jnp.zeros((D,), dtype=jnp.float32), 'Wk': jax.random.normal(ks[4], (D, D), dtype=jnp.float32) * scale, 'bk': jnp.zeros((D,), dtype=jnp.float32), 'Wv': jax.random.normal(ks[5], (D, D), dtype=jnp.float32) * scale, 'bv': jnp.zeros((D,), dtype=jnp.float32), 'Wo': jax.random.normal(ks[6], (D, D), dtype=jnp.float32) * scale, 'bo': jnp.zeros((D,), dtype=jnp.float32)}
        return inp
    _L0_xattn_all = _L0_xattn_setup()
    _L0_xattn_in = {k: v for k, v in _L0_xattn_all.items() if k in ('Wq', 'bq', 'Wk', 'bk', 'Wv', 'bv', 'Wo', 'bo')}
    del _L0_xattn_all

    def _L0_ffn_setup():
        import jax, jax.numpy as jnp
        import numpy as np
        NUM_EXPERTS = 8
        TOP_K = 2
        P_NORM = 1.0
        HIDDEN = 128
        FFN_HIDDEN = 256
        BATCH, SEQ = (2, 256)
        key = jax.random.key(seed)
        ks = jax.random.split(key, 5)
        s = 0.02
        return {'x': jax.random.normal(ks[0], (BATCH, SEQ, HIDDEN), dtype=jnp.float32), 'router_w': jax.random.normal(ks[1], (NUM_EXPERTS, HIDDEN), dtype=jnp.float32) * s, 'w1': jax.random.normal(ks[2], (NUM_EXPERTS, FFN_HIDDEN, HIDDEN), dtype=jnp.float32) * s, 'v1': jax.random.normal(ks[3], (NUM_EXPERTS, FFN_HIDDEN, HIDDEN), dtype=jnp.float32) * s, 'w2': jax.random.normal(ks[4], (NUM_EXPERTS, FFN_HIDDEN, HIDDEN), dtype=jnp.float32) * s}
    _L0_ffn_all = _L0_ffn_setup()
    _L0_ffn_in = {k: v for k, v in _L0_ffn_all.items() if k in ('router_w', 'w1', 'v1', 'w2')}
    del _L0_ffn_all
    return {'x': x, 'ctx_1024': ctx_1024, 'L0_attn_W_in': _L0_attn_in['W_in'], 'L0_attn_conv_w': _L0_attn_in['conv_w'], 'L0_attn_conv_b': _L0_attn_in['conv_b'], 'L0_attn_A_log': _L0_attn_in['A_log'], 'L0_attn_dt_bias': _L0_attn_in['dt_bias'], 'L0_attn_D_skip': _L0_attn_in['D_skip'], 'L0_attn_W_out': _L0_attn_in['W_out'], 'L0_xattn_Wq': _L0_xattn_in['Wq'], 'L0_xattn_bq': _L0_xattn_in['bq'], 'L0_xattn_Wk': _L0_xattn_in['Wk'], 'L0_xattn_bk': _L0_xattn_in['bk'], 'L0_xattn_Wv': _L0_xattn_in['Wv'], 'L0_xattn_bv': _L0_xattn_in['bv'], 'L0_xattn_Wo': _L0_xattn_in['Wo'], 'L0_xattn_bo': _L0_xattn_in['bo'], 'L0_ffn_router_w': _L0_ffn_in['router_w'], 'L0_ffn_w1': _L0_ffn_in['w1'], 'L0_ffn_v1': _L0_ffn_in['v1'], 'L0_ffn_w2': _L0_ffn_in['w2']}

def reference(x, ctx_1024, L0_attn_W_in, L0_attn_conv_w, L0_attn_conv_b, L0_attn_A_log, L0_attn_dt_bias, L0_attn_D_skip, L0_attn_W_out, L0_xattn_Wq, L0_xattn_bq, L0_xattn_Wk, L0_xattn_bk, L0_xattn_Wv, L0_xattn_bv, L0_xattn_Wo, L0_xattn_bo, L0_ffn_router_w, L0_ffn_w1, L0_ffn_v1, L0_ffn_w2):
    import jax
    import jax.numpy as jnp

    def _L0_attn_ref(x, W_in, conv_w, conv_b, A_log, dt_bias, D_skip, W_out):
        import jax, jax.numpy as jnp
        from jax import lax
        import numpy as np
        D_MODEL = 128
        D_STATE = 64
        D_CONV = 4
        EXPAND = 2
        HEADDIM = 128
        NGROUPS = 1
        CHUNK = 32
        D_INNER = EXPAND * D_MODEL
        NHEADS = D_INNER // HEADDIM
        CONV_DIM = D_INNER + 2 * NGROUPS * D_STATE
        D_IN_PROJ = D_INNER + CONV_DIM + NHEADS

        def _segsum_exp(t):
            T = t.shape[-1]
            cs = jnp.cumsum(t, axis=-1)
            d = cs[..., :, None] - cs[..., None, :]
            mask = jnp.tril(jnp.ones((T, T), dtype=bool))
            return jnp.where(mask, jnp.exp(jnp.where(mask, d, 0.0)), 0.0)

        def _ssd_scan(x, dt, A, Bm, Cm, chunk):
            Bz, L, H, P = x.shape
            G, N = (Bm.shape[2], Bm.shape[3])
            nc = L // chunk
            rep = H // G
            Bh = jnp.repeat(Bm, rep, axis=2)
            Ch = jnp.repeat(Cm, rep, axis=2)
            xc = x.reshape(Bz, nc, chunk, H, P)
            dtc = dt.reshape(Bz, nc, chunk, H)
            Bc = Bh.reshape(Bz, nc, chunk, H, N)
            Cc = Ch.reshape(Bz, nc, chunk, H, N)
            dA = dtc * A[None, None, None, :]
            dAh = jnp.transpose(dA, (0, 1, 3, 2))
            A_cs = jnp.cumsum(dAh, axis=-1)
            Lmat = _segsum_exp(dAh)
            Y_diag = jnp.einsum('bcqhn,bckhn,bchqk,bckh,bckhp->bcqhp', Cc, Bc, Lmat, dtc, xc)
            decay_states = jnp.exp(A_cs[..., -1:] - A_cs)
            states = jnp.einsum('bckhn,bchk,bckh,bckhp->bchpn', Bc, decay_states, dtc, xc)
            chunk_total = jnp.transpose(A_cs[..., -1], (0, 2, 1))
            padded = jnp.pad(chunk_total, ((0, 0), (0, 0), (1, 0)))
            decay_chunk = _segsum_exp(padded)
            states_cat = jnp.concatenate([jnp.zeros_like(states[:, :1]), states], axis=1)
            new_states = jnp.einsum('bhzc,bchpn->bzhpn', decay_chunk, states_cat)
            prev = new_states[:, :-1]
            Y_off = jnp.einsum('bcqhn,bchpn,bchq->bcqhp', Cc, prev, jnp.exp(A_cs))
            return (Y_diag + Y_off).reshape(Bz, L, H, P)
        Bz, L, _ = x.shape
        proj = x @ W_in.T
        z = proj[..., :D_INNER]
        xBC = proj[..., D_INNER:D_INNER + CONV_DIM]
        dt_raw = proj[..., D_INNER + CONV_DIM:]
        xBC_t = jnp.transpose(xBC, (0, 2, 1))
        conv = lax.conv_general_dilated(xBC_t, conv_w, (1,), [(D_CONV - 1, 0)], dimension_numbers=('NCH', 'OIH', 'NCH'), feature_group_count=CONV_DIM)
        xBC = jnp.transpose(conv + conv_b[None, :, None], (0, 2, 1))
        xBC = jax.nn.silu(xBC)
        x_ssm = xBC[..., :D_INNER].reshape(Bz, L, NHEADS, HEADDIM)
        B_ssm = xBC[..., D_INNER:D_INNER + NGROUPS * D_STATE].reshape(Bz, L, NGROUPS, D_STATE)
        C_ssm = xBC[..., D_INNER + NGROUPS * D_STATE:].reshape(Bz, L, NGROUPS, D_STATE)
        dt = jax.nn.softplus(dt_raw + dt_bias[None, None, :])
        A = -jnp.exp(A_log)
        y = _ssd_scan(x_ssm, dt, A, B_ssm, C_ssm, CHUNK)
        y = y + x_ssm * D_skip[None, None, :, None]
        y = y.reshape(Bz, L, D_INNER)
        y = y * jax.nn.silu(z)
        return y @ W_out.T

    def _L0_xattn_ref(query, key, value, Wq, bq, Wk, bk, Wv, bv, Wo, bo):
        import jax, jax.numpy as jnp
        import numpy as np
        EMBED = 128
        HEADS = 16
        HEAD_DIM = EMBED // HEADS
        B, S, D = query.shape
        H, Dh = (HEADS, HEAD_DIM)

        def proj(x, W, b):
            y = jnp.einsum('bsd,ed->bse', x, W) + b
            return y.reshape(B, -1, H, Dh).transpose(0, 2, 1, 3)
        q = proj(query, Wq, bq)
        k = proj(key, Wk, bk)
        v = proj(value, Wv, bv)
        attn = jnp.einsum('bhqd,bhkd->bhqk', q, k) / jnp.sqrt(jnp.float32(Dh))
        attn = jax.nn.softmax(attn, axis=-1)
        out = jnp.einsum('bhqk,bhkd->bhqd', attn, v)
        out = out.transpose(0, 2, 1, 3).reshape(B, -1, D)
        out = jnp.einsum('bsd,ed->bse', out, Wo) + bo
        return out

    def _L0_ffn_ref(x, router_w, w1, v1, w2):
        import jax, jax.numpy as jnp
        import numpy as np
        NUM_EXPERTS = 8
        TOP_K = 2
        P_NORM = 1.0
        HIDDEN = 128
        FFN_HIDDEN = 256
        BATCH, SEQ = (2, 256)
        B, S, H = x.shape
        xf = x.reshape(-1, H)
        logits = xf @ router_w.T
        probs = jax.nn.softmax(logits.astype(jnp.float32), axis=-1)
        top_w, top_e = jax.lax.top_k(probs, TOP_K)
        norm = jnp.sum(jnp.abs(top_w) ** P_NORM, axis=-1, keepdims=True) ** (1.0 / P_NORM)
        top_w = (top_w / norm).astype(x.dtype)
        c = jnp.sum(jax.nn.one_hot(top_e, NUM_EXPERTS, dtype=x.dtype) * top_w[..., None], axis=1)
        out = jnp.zeros_like(xf)
        for e in range(NUM_EXPERTS):
            h = jax.nn.silu(xf @ w1[e].T) * (xf @ v1[e].T)
            out = out + h @ w2[e] * c[:, e:e + 1]
        return out.reshape(B, S, H)
    x = _layernorm(x + _L0_attn_ref(x, L0_attn_W_in, L0_attn_conv_w, L0_attn_conv_b, L0_attn_A_log, L0_attn_dt_bias, L0_attn_D_skip, L0_attn_W_out), axis=-1)
    x = _layernorm(x + _L0_xattn_ref(x, ctx_1024, ctx_1024, L0_xattn_Wq, L0_xattn_bq, L0_xattn_Wk, L0_xattn_bk, L0_xattn_Wv, L0_xattn_bv, L0_xattn_Wo, L0_xattn_bo), axis=-1)
    x = _layernorm(x + _L0_ffn_ref(x, L0_ffn_router_w, L0_ffn_w1, L0_ffn_v1, L0_ffn_w2), axis=-1)
    return x

_drawn_inputs = setup_inputs


def setup_inputs(seed=0):
    import zlib

    import numpy as np

    out = dict(_drawn_inputs(seed))
    spreads = {'L0_attn_conv_b': (0.0, 0.8),
     'L0_attn_D_skip': (1.0, 0.6),
     'L0_xattn_bq': (0.0, 0.348),
     'L0_xattn_bk': (0.0, 0.8),
     'L0_xattn_bv': (0.0, 0.1),
     'L0_xattn_bo': (0.0, 0.1)}
    factors = {'L0_attn_W_in': 8.0,
     'L0_attn_conv_w': 8.0,
     'L0_attn_A_log': 8.0,
     'L0_attn_dt_bias': 8.0,
     'L0_attn_W_out': 8.0,
     'L0_ffn_router_w': 8.0,
     'L0_ffn_w1': 8.0,
     'L0_ffn_v1': 8.0,
     'L0_ffn_w2': 8.0}
    for name, (base, spread) in spreads.items():
        noise = np.random.default_rng([zlib.crc32(name.encode()), seed]).standard_normal(out[name].shape)
        drawn = base * np.exp(spread * noise) if base else spread * noise
        out[name] = jnp.asarray(drawn.astype(out[name].dtype))
    for name, factor in factors.items():
        out[name] = (out[name] * factor).astype(out[name].dtype)
    return out
```

```python
from contextlib import ExitStack

import numpy as np
import concourse.bass as bass
from concourse import mybir

F32 = mybir.dt.float32
F32R = mybir.dt.float32r
U32 = mybir.dt.uint32
ALU = mybir.AluOpType
ACT = mybir.ActivationFunctionType
AX = mybir.AxisListType

P = 128
NB, L, D = 4, 512, 128
NT = L // P
NS = 64
NC = 3
TAPS = 4
NH = 2
HA, DH, G, J = 16, 8, 4, 4
S = 77
E, FC = 8, 2
U = E * FC
EPS = 1e-5
UNDERFLOW = -110.0
LOG_TERMS = 8
SCALE = float(DH) ** -0.5
CW, CB, ALOG, DTB, DSK, BQ, BK, BV = 0, 12, 15, 17, 19, 21, 25, 29
NSMALL = 30
IDENT, TRI, LAST, ONES, MQ, MK, KEEP, IND, SELC, IOTA = 0, 128, 256, 384, 512, 513, 514, 515, 531, 539
NCST = 547
WZ, WX, WDT = 0, 256, 640


def constants():
    c = np.zeros((P, NCST), np.float32)
    p = np.arange(P)
    c[:, IDENT:IDENT + P] = np.eye(P)
    c[:, TRI:TRI + P] = p[:, None] <= p[None, :]
    c[P - 1, LAST:LAST + P] = 1.0
    for g in range(G):
        c[:S, ONES + 32 * g + 8 * g:ONES + 32 * g + 8 * g + 8] = 1.0
    r = p % 32
    c[:, MQ] = -1.0 * ((r >= 8) & (r < 16))
    c[:, MK] = -1.0 * ((r >= 16) & (r < 24))
    c[:, KEEP] = r < 24
    for h in range(HA):
        c[h, IND + h] = c[HA + h, IND + h] = -1.0
    for e in range(E):
        c[e, SELC + e] = c[E + e, SELC + e] = 1.0
    c[:, IOTA:IOTA + E] = np.arange(E)
    return c


def decoder_kernel(nc, x_feat, x_tok, ctx_feat, small, cst, bo_row, w_in, w_out, wq, wk, wv, wo,
                   router, w1, v1, w2, out):
    with ExitStack() as ctx:
        def sb(name, shape, dt=F32):
            return ctx.enter_context(nc.sbuf_tensor(name, shape, dt))

        def sem(name):
            return ctx.enter_context(nc.semaphore(name))

        xfH = sb("xfH", [P, NB * L], F32R)
        xfL = sb("xfL", [P, NB * L], F32R)
        sm = sb("sm", [P, NSMALL])
        con = sb("con", [P, NCST])
        bo = sb("bo", [P, D])
        winH = sb("winH", [P, 640], F32R)
        winL = sb("winL", [P, 640], F32R)
        wout = sb("wout", [P, NH, D])
        wqH = sb("wqH", [P, G * P], F32R)
        wqL = sb("wqL", [P, G * P], F32R)
        wvs = sb("wvs", [P, D])
        wos = sb("wos", [P, D])
        wr = sb("wr", [P, E])
        w1H = sb("w1H", [P, 2, E * FC * P], F32R)
        w1L = sb("w1L", [P, 2, E * FC * P], F32R)
        w2s = sb("w2s", [P, E * FC, D])
        ident = con[:, IDENT:IDENT + P]
        tri = con[:, TRI:TRI + P]
        last = con[:, LAST:LAST + P]
        ones = con[:, ONES:ONES + P]
        cwh = sb("cwh", [P, NC * TAPS + NC])
        sel = sb("sel", [P, HA + E], F32R)
        aexp = sb("aexp", [P, NH])
        dtx = sb("dtx", [P, 5, NB * NT * NH])
        dta = sb("dta", [P, NB * NT * NH])
        sc = sb("sc", [P, NB, 4, NT * NH])
        kc = sb("kc", [P, NB, G, S], F32R)
        vc = sb("vc", [S, NB, D])
        half = sb("half", [P, NT])
        kst = sb("kst", [P, HA, S], F32R)
        vst = sb("vst", [P, HA, 32])
        scb = sb("scb", [P, 4, NT * NH])
        xt = sb("xt", [P, NT, D])
        raw = sb("raw", [P, NC, TAPS - 1 + L])
        acc = sb("acc", [P, NC, L])
        xs = sb("xs", [P, NC, L])
        gz = sb("gz", [P, NH, L])
        dd = sb("dd", [P, NH, L])
        bw = sb("bw", [P, NH, NT - 1, NS])
        st = sb("st", [NS, NH, NT - 1, D])
        res = [sb(f"res{k}", [P, NT, D]) for k in range(3)]
        bst = sb("bst", [P, 3, NT, 6])
        mv = sb("mv", [P, 3, NT, 2])
        rstd = sb("rstd", [P, 3, 2, NT])
        x1 = sb("x1", [P, NT, D])
        x1H = sb("x1H", [P, L], F32R)
        x1L = sb("x1L", [P, L], F32R)
        qst = sb("qst", [P, G, L], F32R)
        smax = sb("smax", [P, NT, HA])
        smH = sb("smH", [P, NT, HA], F32R)
        smHL = sb("smHL", [P, NT, 2, HA])
        mt = sb("mt", [P, L], F32R)
        pr = sb("pr", [P, 2, J, L])
        rsum = sb("rsum", [P, L])
        att = sb("att", [P, L])
        x2 = sb("x2", [P, NB, NT, D])
        x2H = sb("x2H", [P, L], F32R)
        x2L = sb("x2L", [P, L], F32R)
        lg = sb("lg", [P, 6, NT, E])
        lmx = sb("lmx", [P, 4, NT])
        top = sb("top", [P, NT, 8])
        topi = sb("topi", [P, NT, 8], U32)
        topf = sb("topf", [P, NT, 8])
        cH = sb("cH", [P, NT, E], F32R)
        cHL = sb("cHL", [P, NT, 2, E])
        ct = sb("ct", [P, L], F32R)
        cb = sb("cb", [P, E, L])
        mt_u = sb("moe_u", [P, 2, L])
        mt_h = sb("moe_h", [P, 2, L])
        xf = x2[:, :, :, :].rearrange("p b t d -> p (b t d)")
        win = gz[:, :, :].rearrange("p h l -> p (h l)")[:, 0:642]
        wqk = dd
        wkH, wkL, cxH, cxL = qst[:, 0, :], qst[:, 1, :], qst[:, 2, 0:NB * S], qst[:, 3, 0:NB * S]
        cx = res[0][:, :, :].rearrange("p t d -> p (t d)")[:, 0:NB * S]
        k32 = x1[:, :, :].rearrange("p t d -> p (t d)")[:, 0:NB * S]
        kst0 = res[1][:, :, :].rearrange("p t d -> p (t d)")[:, 0:NB * S]
        kH = x1H[:, 0:NB * S]
        w1s = cb[:, :, :].rearrange("p e l -> p (e l)").rearrange("p (w k) -> p w k", w=2)
        y1 = acc
        ecs = pr[0:NS, 0, 0:NH, :]
        clow = pr[0:NS, 0, NH, :]
        gm = x2c = rsum
        q32 = dd
        x1bo = res[0]
        yt = att

        def xtok(h, c):
            return raw[:, h, TAPS - 1 + c * P:TAPS - 1 + (c + 1) * P]

        F = [ctx.enter_context(nc.psum_tensor(f"front{i}", [P, 512], F32)) for i in range(4)]
        M = [ctx.enter_context(nc.psum_tensor(f"moe{i}", [P, 512], F32)) for i in range(3)]
        Y = ctx.enter_context(nc.psum_tensor("moe_y", [P, 512], F32))

        ld_x, ld_tok, ld_late, ld_ctx, ld_w, ld_c, ld_moe = (sem(n) for n in (
            "ld_x", "ld_tok", "ld_late", "ld_ctx", "ld_w", "ld_c", "ld_moe"))
        c_low, stored = sem("c_low"), sem("stored")
        su = {n: sem(f"su_{n}") for n in (
            "high", "low", "taps", "dt_p", "dt_x", "dt_neg", "dt_exp", "log1p", "dt", "dta", "aexp",
            "cs_p", "cs", "end_p", "end_d", "end_exp", "end_w", "total", "key_p", "key32", "keyH",
            "keyS", "key_in", "val_p", "val_in", "zero", "sel", "moeH", "moeL", "half")}

        counts = dict(
            proj=5, csb=2, xtT=2, btT=1, gdot=1, upd=2, ydot=2, wout_d=1, x1T=1, qdot=4, tsc=16,
            mT=1, ksc=8, pv=4, wo_d=1, x2T=1, logit=1, cT=1, cbd=8, ab=2 * U, w2d=U, yT=1,
            raw_c=3, tap0=3, tanh_c=3, tanh_z=2, ecs_r=2, dec=2, xtok_r=2, x1h=1, q32_r=4, mt_r=1,
            prob=8, attb_r=1, x2h=1, x2c_r=1, lexp=1, ct_r=1, cbs=8, tanh_m=U, yt_r=1,
            conv=9, xs_r=3, gz_r=2, dd_r=8, bw_r=6, gm_r=1, m_r=8, s_r=6, y1_r=2,
            res0=1, res1=1, res2=1, stat0=4, stat1=4, stat2=4, mv0=4, mv1=4, mv2=4,
            norm0=4, norm1=4, norm2=4, x1l=1, qh_r=4, qst_r=4, tmax=16, msplit=3,
            att_r=1, rs_r=1, x2l=1, lgv=13, topv=16, moe_u=U, moe_h0=U,
            copies=9, kept=1, csd_r=2, yg_r=2, bo_r=1, eps0=1, eps1=1, eps2=1, rstd0=1, rstd1=1, rstd2=1,
            moe_h=U,
        )
        done = {n: sem(n) for n in counts}

        def reach(eng, name, b, k, alone=False):
            if k <= 0:
                return
            v = counts[name] * b + k
            if not isinstance(v, int):
                if alone:
                    v = eng.to_reg(v)
                    eng.wait_ge(ld_c, 32)
                eng.wait_ge(done[name], v)
            elif v > 0:
                eng.wait_ge(done[name], v)

        def row(b):
            return bass.ds(b * L, L)

        block = ctx.enter_context(nc.Block())
        AT_CONV, AT_SCAN, AT_NORM1, AT_MAX, AT_SCORE, AT_NORM2 = (
            range(0, 3), range(3, 5), range(5, 7), range(7, 8), range(8, 14), range(14, 16))

        @block.sync
        def _(sp):
            sp.dma_start(win, w_in).then_inc(ld_w, 16)
            sp.dma_start(con[:, :], cst).then_inc(ld_c, 16)
            sp.dma_start(sm[:, :], small).then_inc(ld_c, 16)
            sp.dma_start(xf, x_feat).then_inc(ld_x, 16)
            sp.dma_start(cx, ctx_feat).then_inc(ld_ctx, 16)
            sp.dma_start(wqk[:, 1, :], wk).then_inc(ld_ctx, 16)
            sp.dma_start(wqk[:, 0, :], wq).then_inc(ld_ctx, 16)
            sp.dma_start(wvs[:, :], wv).then_inc(ld_ctx, 16)
            sp.dma_start(wout[:, :, :], w_out).then_inc(ld_late, 16)
            sp.dma_start(bo[:, :], bo_row).then_inc(ld_late, 16)
            sp.dma_start(wos[:, :], wo).then_inc(ld_late, 16)
            sp.dma_start(wr[:, :], router).then_inc(ld_late, 16)
            sp.dma_start(w1s[:, 0, :], w1).then_inc(ld_moe, 16)
            sp.dma_start(w1s[:, 1, :], v1).then_inc(ld_moe, 16)
            sp.dma_start(w2s[:, :, :], w2).then_inc(ld_moe, 16)

            def load_tokens(b):
                reach(sp, "res0", b - 1, 1)
                sp.dma_start(xt[:, :, :], x_tok[:, b, :, :]).then_inc(ld_tok, 16)

            def lower_c(b):
                reach(sp, "csd_r", b - 1, 2)
                reach(sp, "gdot", b - 1, 1)
                reach(sp, "xs_r", b, 3)
                sp.dma_start(clow[:, :], xs[NS:P, 2, :]).then_inc(c_low, 16)

            def store(b):
                reach(sp, "norm2", b, 4)
                sp.dma_start(out[:, b, :, :], x2[:, b, :, :]).then_inc(stored, 16)

            load_tokens(0)
            lower_c(0)
            with sp.Fori(1, NB) as b:
                load_tokens(b)
                lower_c(b)
                store(b - 1)
            store(NB - 1)
            sp.wait_ge(stored, 16 * NB)

        @block.tensor
        def _(pe):
            def split3(o, wH, wL, xH, xL, signal):
                pe.matmul(o, wH, xH, start=True, stop=False)
                pe.matmul(o, wH, xL, start=False, stop=False)
                pe.matmul(o, wL, xH, start=False, stop=True).then_inc(signal, 1)

            def setup():
                pe.wait_ge(ld_x, 16)
                pe.wait_ge(ld_w, 16)
                for t in range(NB * NT):
                    mm = pe.matmul(F[0][:, NH * t:NH * t + NH], xf[:, t * P:(t + 1) * P],
                                   win[:, WDT:WDT + NH], start=True, stop=True)
                mm.then_inc(su["dt_p"], 1)
                pe.wait_ge(ld_c, 32)
                pe.wait_ge(su["dta"], 2)
                pe.matmul(F[1][:, 0:NB * NT * NH], tri, dta[:, :], start=True, stop=True).then_inc(su["cs_p"], 1)
                pe.wait_ge(su["cs"], 1)
                pe.matmul(F[2][:, 0:NB * NT * NH].rearrange("p (b c) -> p b c", b=NB), last,
                          sc[:, :, 0, :], start=True, stop=True).then_inc(su["end_p"], 1)
                pe.wait_ge(su["high"], 6)
                pe.wait_ge(su["low"], 6)
                pe.wait_ge(su["end_d"], 1)
                pe.wait_ge(su["total"], 1)
                for g in range(G):
                    split3(F[g][:, 0:NB * S], wkH[:, g * P:(g + 1) * P], wkL[:, g * P:(g + 1) * P],
                           cxH, cxL, su["key_p"])
                for b in range(NB):
                    mm = pe.matmul(M[0][0:S, b * D:(b + 1) * D], cx[:, b * S:(b + 1) * S], wvs[:, :],
                                   start=True, stop=True)
                mm.then_inc(su["val_p"], 1)

            def unit(m, u):
                e, f = divmod(u, FC)
                for which in range(2):
                    k = 2 * u + which
                    if k >= 3:
                        reach(pe, "moe_u" if (k - 3) % 2 == 0 else "moe_h0", m, (k - 3) // 2 + 1)
                    w = slice(u * P, (u + 1) * P)
                    split3(M[k % 3][:, :], w1H[:, which, w], w1L[:, which, w], x2H[:, :], x2L[:, :], done["ab"])
                if u > 0:
                    down(m, u - 1)

            def down(m, u):
                reach(pe, "moe_h", m, u + 1)
                pe.matmul(Y[:, :], w2s[:, u, :], mt_h[:, u % 2, :], start=(u == 0),
                          stop=(u == U - 1)).then_inc(done["w2d"], 1)

            def experts_end(m):
                down(m, U - 1)
                reach(pe, "yt_r", m, 1)
                for t in range(NT):
                    mm = pe.transpose(M[0][:, t * P:(t + 1) * P], yt[:, t * P:(t + 1) * P], ident)
                mm.then_inc(done["yT"], 1)

            def units(m, which):
                if m is not None:
                    for u in which:
                        unit(m, u)

            def front(b, m):
                reach(pe, "cbs", b - 1, 8)
                for i, col in enumerate((WX, WX + P, WX + 2 * P, WZ, WZ + P)):
                    if i == 4:
                        reach(pe, "tap0", b, 1)
                    split3(F[i % 4][:, :], winH[:, col:col + P], winL[:, col:col + P],
                           xfH[:, row(b)], xfL[:, row(b)], done["proj"])
                reach(pe, "copies", b, 1)
                for h in range(NH):
                    reach(pe, "tap0", b, 2 + h)
                    for c in range(NT):
                        col = scb[:, 0, NH * c + h:NH * c + h + 1]
                        mm = pe.matmul(F[1 + h][:, c * P:(c + 1) * P], col.to_broadcast([P, P]), ident,
                                       start=True, stop=True)
                    mm.then_inc(done["csb"], 1)
                units(m, AT_CONV)
                for h in range(NH):
                    reach(pe, "xs_r", b, h + 1)
                    reach(pe, "gz_r", b, h + 1)
                    for c in range(NT):
                        mm = pe.transpose(F[(3, 0)[h]][:, c * P:(c + 1) * P], xs[:, h, c * P:(c + 1) * P], ident)
                    mm.then_inc(done["xtT"], 1)
                reach(pe, "xs_r", b, 3)
                reach(pe, "dd_r", b, 4, alone=True)
                reach(pe, "ecs_r", b, 1, alone=True)
                for c in range(NT - 1):
                    mm = pe.transpose(F[1][:, c * NS:(c + 1) * NS], xs[0:NS, 2, c * P:(c + 1) * P], ident[0:NS, 0:NS])
                mm.then_inc(done["btT"], 1)
                pe.wait_ge(c_low, 16 * (b + 1))
                reach(pe, "dd_r", b, 8)
                reach(pe, "ecs_r", b, 2)
                for c in range(NT):
                    mm = pe.matmul(F[2][:, c * P:(c + 1) * P], xs[0:NS, 2, c * P:(c + 1) * P],
                                   clow[:, c * P:(c + 1) * P], start=True, stop=True)
                mm.then_inc(done["gdot"], 1)
                units(m, AT_SCAN)
                reach(pe, "bw_r", b, 6)
                reach(pe, "xtok_r", b, 2)
                for h in range(NH):
                    for c in range(NT - 1):
                        mm = pe.matmul(F[(1, 3)[h]][0:NS, c * P:(c + 1) * P], bw[:, h, c, :],
                                       xtok(h, c), start=True, stop=True)
                    mm.then_inc(done["upd"], 1)
                for h in range(NH):
                    reach(pe, "m_r", b, 4 * h + 4)
                    reach(pe, "csd_r", b, h + 1)
                    for c in range(NT):
                        o = F[(0, 2)[h]][:, c * P:(c + 1) * P]
                        mm = pe.matmul(o, xtok(h, c), dd[:, h, c * P:(c + 1) * P],
                                       start=True, stop=(c == 0))
                        if c:
                            reach(pe, "s_r", b, NH * c if c < NT - 1 else 6)
                            mm = pe.matmul(o, st[:, h, c - 1, :], ecs[:, h, c * P:(c + 1) * P],
                                           start=False, stop=True)
                    mm.then_inc(done["ydot"], 1)
                reach(pe, "yg_r", b, 2)
                for t in range(NT):
                    for h in range(NH):
                        mm = pe.matmul(F[1][:, t * D:(t + 1) * D], y1[:, h, t * P:(t + 1) * P],
                                       wout[:, h, :], start=(h == 0), stop=(h == NH - 1))
                mm.then_inc(done["wout_d"], 1)
                units(m, AT_NORM1)
                reach(pe, "norm0", b, 4)
                for t in range(NT):
                    mm = pe.transpose(F[3][:, t * P:(t + 1) * P], x1[:, t, :], ident)
                mm.then_inc(done["x1T"], 1)
                reach(pe, "x1h", b, 1)
                reach(pe, "x1l", b, 1)
                for g in range(G):
                    split3(F[g][:, :], wqH[:, g * P:(g + 1) * P], wqL[:, g * P:(g + 1) * P],
                           x1H[:, :], x1L[:, :], done["qdot"])
                reach(pe, "copies", b, 5)
                for i in range(NT * G):
                    t, g = divmod(i, G)
                    if t == 0:
                        reach(pe, "qst_r", b, g + 1)
                    else:
                        reach(pe, "tmax", b, i - 3)
                    pe.matmul(F[g][:, 0:J * S], qst[:, g, t * P:(t + 1) * P],
                              kst[:, J * g:J * g + J, :].rearrange("p j s -> p (j s)"),
                              start=True, stop=True).then_inc(done["tsc"], 1)
                units(m, AT_MAX)
                reach(pe, "msplit", b, 3)
                for t in range(NT):
                    mm = pe.transpose(F[0][0:2 * HA, t * P:(t + 1) * P],
                                      smHL[:, t, :, :].rearrange("p k h -> p (k h)"), ident)
                mm.then_inc(done["mT"], 1)
                reach(pe, "mt_r", b, 1)

                def scores(p):
                    reach(pe, "prob", b, p)
                    for i in range(2):
                        h = 2 * p + i
                        pe.matmul(F[i][0:S, :], kst[:, h, :], qst[:, h // J, :], start=True, stop=False)
                        mm = pe.matmul(F[i][0:S, :], sel[:, h:h + 1].to_broadcast([P, S]), mt[:, :], start=False, stop=True)
                    mm.then_inc(done["ksc"], 1)

                def values(g):
                    reach(pe, "prob", b, 2 * g + 2)
                    if g == 0:
                        reach(pe, "copies", b, 9)
                    for o, w in ((F[2], lambda h: vst[:, h, :]), (F[3], lambda h: ones[:, 32 * g:32 * g + 32])):
                        for j in range(J):
                            mm = pe.matmul(o[32 * j:32 * j + 32, :], w(J * g + j), pr[:, g % 2, j, :],
                                           start=(g == 0), stop=(g == G - 1))
                    mm.then_inc(done["pv"], 1)

                scores(0)
                for p in range(1, 8):
                    if p - 1 < len(AT_SCORE):
                        units(m, AT_SCORE[p - 1:p])
                    scores(p)
                    if p % 2 == 0:
                        values(p // 2 - 1)
                values(G - 1)
                reach(pe, "attb_r", b, 1)
                for t in range(NT):
                    mm = pe.matmul(F[0][:, t * D:(t + 1) * D], att[:, t * P:(t + 1) * P], wos[:, :],
                                   start=True, stop=True)
                mm.then_inc(done["wo_d"], 1)
                units(m, AT_NORM2)
                reach(pe, "norm1", b, 4)
                for t in range(NT):
                    mm = pe.transpose(F[1][:, t * P:(t + 1) * P], res[1][:, t, :], ident)
                mm.then_inc(done["x2T"], 1)
                if m is not None:
                    experts_end(m)
                reach(pe, "x2c_r", b, 1)
                for t in range(NT):
                    mm = pe.matmul(F[0][:, t * E:(t + 1) * E], x2c[:, t * P:(t + 1) * P], wr[:, :],
                                   start=True, stop=True)
                mm.then_inc(done["logit"], 1)
                reach(pe, "lgv", b, 13)
                for t in range(NT):
                    mm = pe.transpose(F[2][0:2 * E, t * P:(t + 1) * P],
                                      cHL[:, t, :, :].rearrange("p k e -> p (k e)"), ident)
                mm.then_inc(done["cT"], 1)
                reach(pe, "ct_r", b, 1)
                reach(pe, "x2l", b, 1)
                for e in range(E):
                    if e >= 2:
                        reach(pe, "cbs", b, e - 1)
                    pe.matmul(F[(3, 1)[e % 2]][:, :], sel[:, HA + e:HA + e + 1].to_broadcast([P, P]), ct[:, :], start=True,
                              stop=True).then_inc(done["cbd"], 1)

            setup()
            pe.wait_ge(su["key32"], G)
            pe.wait_ge(ld_late, 64)
            pe.wait_ge(su["zero"], 6)
            pe.wait_ge(su["sel"], 1)
            front(0, None)
            pe.wait_ge(su["val_in"], 1)
            pe.wait_ge(su["moeH"], 2)
            pe.wait_ge(su["moeL"], 2)
            pe.wait_ge(ld_moe, 48)
            with pe.Fori(1, NB) as b:
                front(b, b - 1)
            for u in range(U):
                unit(NB - 1, u)
            experts_end(NB - 1)

        @block.scalar
        def _(act):
            def setup():
                act.wait_ge(ld_w, 16)
                act.activation(winH[:, WZ:WX], win[:, WZ:WX], ACT.Copy, scale=0.5).then_inc(su["high"], 1)
                act.activation(winH[:, WX:WDT], win[:, WX:WDT], ACT.Copy).then_inc(su["high"], 1)
                act.wait_ge(ld_x, 16)
                act.activation(xfH[:, :], xf[:, :], ACT.Copy).then_inc(su["high"], 1)
                act.wait_ge(ld_c, 32)
                act.activation(aexp[:, :], sm[:, ALOG:ALOG + NH], ACT.Exp).then_inc(su["aexp"], 1)
                act.wait_ge(su["dt_neg"], 1)
                act.activation(dtx[:, 1, :], dtx[:, 1, :], ACT.Exp).then_inc(su["dt_exp"], 1)
                act.wait_ge(su["end_d"], 1)
                act.activation(sc[:, :, 2, :], sc[:, :, 2, :], ACT.Exp).then_inc(su["end_exp"], 1)
                act.wait_ge(su["end_p"], 1)
                act.activation(sc[:, :, 3, :], F[2][:, 0:NB * NT * NH].rearrange("p (b c) -> p b c", b=NB),
                               ACT.Exp).then_inc(su["total"], 1)
                act.wait_ge(ld_ctx, 64)
                act.activation(cxH, cx, ACT.Copy).then_inc(su["high"], 1)
                act.activation(wkH, wqk[:, 1, :], ACT.Copy).then_inc(su["high"], 1)
                act.activation(wqH[:, :], wqk[:, 0, :], ACT.Copy).then_inc(su["high"], 1)
                for g in range(G):
                    act.wait_ge(su["key_p"], g + 1)
                    if g:
                        act.wait_ge(su["keyS"], g)
                    act.activation(k32, F[g][:, 0:NB * S], ACT.Identity,
                                   bias=sm[:, BK + g:BK + g + 1]).then_inc(su["key32"], 1)
                act.wait_ge(su["taps"], 1)

            def setup_experts():
                act.wait_ge(ld_moe, 48)
                act.activation(w1H[:, 0, :], w1s[:, 0, :], ACT.Copy, scale=0.5).then_inc(su["moeH"], 1)
                act.activation(w1H[:, 1, :], w1s[:, 1, :], ACT.Copy).then_inc(su["moeH"], 1)

            def unit(m, u):
                reach(act, "ab", m, 2 * u + 1)
                reach(act, "moe_u", m, u - 1)
                act.activation(mt_u[:, u % 2, :], M[2 * u % 3][:, :], ACT.Tanh).then_inc(done["tanh_m"], 1)

            def units(m, which):
                if m is not None:
                    for u in which:
                        unit(m, u)

            def experts_end(m):
                reach(act, "w2d", m, U)
                act.copy(yt[:, :], Y[:, :]).then_inc(done["yt_r"], 1)

            def front(b, m):
                for i in range(NC):
                    reach(act, "proj", b, i + 1)
                    reach(act, "conv", b - 1, 9)
                    act.activation(raw[:, i, TAPS - 1:], F[i][:, :], ACT.Copy).then_inc(done["raw_c"], 1)
                    reach(act, "xs_r", b - 1, 3)
                    act.activation(acc[:, i, :], F[i][:, :], ACT.Identity,
                                   bias=cwh[:, NC * TAPS + i:NC * TAPS + i + 1],
                                   scale=cwh[:, TAPS * i + 3:TAPS * i + 4]).then_inc(done["tap0"], 1)
                for h in range(NH):
                    reach(act, "proj", b, 4 + h)
                    reach(act, "gz_r", b - 1, 2)
                    act.activation(gz[:, h, :], F[(3, 0)[h]][:, :], ACT.Tanh).then_inc(done["tanh_z"], 1)
                for h in range(NH):
                    reach(act, "csb", b, h + 1)
                    reach(act, "csd_r", b - 1, 2)
                    act.activation(ecs[:, h, :], F[1 + h][0:NS, :], ACT.Exp).then_inc(done["ecs_r"], 1)
                for i in range(NC):
                    reach(act, "conv", b, 7 + i)
                    act.activation(xs[:, i, :], acc[:, i, :], ACT.Tanh).then_inc(done["tanh_c"], 1)
                for h in range(NH):
                    reach(act, "dd_r", b, 4 * h + 4)
                    act.activation(dd[:, h, :], dd[:, h, :], ACT.Exp).then_inc(done["dec"], 1)
                units(m, AT_CONV)
                for h in range(NH):
                    reach(act, "xtT", b, h + 1)
                    act.copy(raw[:, h, TAPS - 1:], F[(3, 0)[h]][:, :]).then_inc(done["xtok_r"], 1)
                units(m, AT_SCAN)
                units(m, AT_NORM1)
                reach(act, "x1T", b, 1)
                act.activation(x1H[:, :], F[3][:, :], ACT.Copy).then_inc(done["x1h"], 1)
                for g in range(G):
                    reach(act, "qdot", b, g + 1)
                    reach(act, "qst_r", b, g - 1)
                    act.activation(q32[:, g % 2, :], F[g][:, :], ACT.Identity,
                                   bias=sm[:, BQ + g:BQ + g + 1]).then_inc(done["q32_r"], 1)
                units(m, AT_MAX)
                reach(act, "mT", b, 1)
                act.activation(mt[0:2 * HA, :], F[0][0:2 * HA, :], ACT.Copy).then_inc(done["mt_r"], 1)
                for p in range(8):
                    if 0 <= p - 1 < len(AT_SCORE):
                        units(m, AT_SCORE[p - 1:p])
                    reach(act, "ksc", b, p + 1)
                    g, j = divmod(2 * p, J)
                    if g >= 2:
                        reach(act, "pv", b, g - 1)
                    for i in range(2):
                        a = act.activation(pr[0:S, g % 2, j + i, :], F[i][0:S, :], ACT.Exp, scale=SCALE)
                    a.then_inc(done["prob"], 1)
                reach(act, "att_r", b, 1)
                act.activation(att[:, :], att[:, :], ACT.Identity, bias=sm[:, BV:BV + 1]).then_inc(done["attb_r"], 1)
                units(m, AT_NORM2)
                reach(act, "x2T", b, 1)
                act.copy(x2c[:, :], F[1][:, :]).then_inc(done["x2c_r"], 1)
                act.activation(x2H[:, :], F[1][:, :], ACT.Copy).then_inc(done["x2h"], 1)
                if m is not None:
                    experts_end(m)
                reach(act, "lgv", b, 2)
                act.activation(lg[:, 1, :, :], lg[:, 0, :, :], ACT.Exp).then_inc(done["lexp"], 1)
                reach(act, "cT", b, 1)
                act.activation(ct[0:2 * E, :], F[2][0:2 * E, :], ACT.Copy).then_inc(done["ct_r"], 1)
                for e in range(E):
                    reach(act, "cbd", b, e + 1)
                    if e == 0 and m is not None:
                        reach(act, "moe_h", m, U)
                    elif e == 0:
                        act.wait_ge(su["moeL"], 2)
                    act.copy(cb[:, e, :], F[(3, 1)[e % 2]][:, :]).then_inc(done["cbs"], 1)

            setup()
            setup_experts()
            front(0, None)
            with act.Fori(1, NB) as b:
                front(b, b - 1)
            for u in range(U):
                unit(NB - 1, u)
            experts_end(NB - 1)

        @block.vector
        def _(dve):
            def f32(ap):
                return ap.bitcast(F32)

            def over(ap, n):
                return ap.unsqueeze(1).broadcast_to([ap.shape[0], n, ap.shape[1]])

            def log1p():
                u, s, z, r = dtx[:, 1, :], dtx[:, 2, :], dtx[:, 3, :], dtx[:, 4, :]
                steps = [0]

                def then(i):
                    i.then_inc(su["log1p"], 1)
                    steps[0] += 1
                    dve.wait_ge(su["log1p"], steps[0])

                dve.wait_ge(su["dt_exp"], 1)
                then(dve.tensor_scalar(z, u, 2.0, None, ALU.add))
                then(dve.reciprocal(z, z))
                then(dve.tensor_tensor(s, u, z, ALU.mult))
                then(dve.tensor_tensor(z, s, s, ALU.mult))
                then(dve.tensor_scalar(r, z, 1.0 / (2 * LOG_TERMS + 1), None, ALU.mult))
                for k in range(LOG_TERMS - 1, 0, -1):
                    then(dve.scalar_tensor_tensor(r, r, 1.0 / (2 * k + 1), z, ALU.add, ALU.mult))
                then(dve.tensor_scalar(r, r, 1.0, 2.0, ALU.add, ALU.mult))
                then(dve.tensor_tensor(u, r, s, ALU.mult))

            def setup():
                dve.wait_ge(ld_c, 32)
                dve.tensor_scalar(cwh[:, :], sm[:, CW:CW + NC * TAPS + NC], 0.5, None, ALU.mult).then_inc(su["taps"], 1)
                dve.wait_ge(su["high"], 2)
                dve.scalar_tensor_tensor(winL[:, WZ:WX], win[:, WZ:WX], 0.5, f32(winH[:, WZ:WX]),
                                         ALU.mult, ALU.subtract).then_inc(su["low"], 1)
                dve.tensor_tensor(winL[:, WX:WDT], win[:, WX:WDT], f32(winH[:, WX:WDT]), ALU.subtract).then_inc(su["low"], 1)
                dve.wait_ge(su["dt_p"], 1)
                dve.tensor_tensor(dtx[:, 0, :].rearrange("p (t h) -> p t h", h=NH),
                                  F[0][:, 0:NB * NT * NH].rearrange("p (t h) -> p t h", h=NH),
                                  over(sm[:, DTB:DTB + NH], NB * NT), ALU.add).then_inc(su["dt_x"], 1)
                dve.wait_ge(su["dt_x"], 1)
                dve.scalar_tensor_tensor(dtx[:, 1, :], dtx[:, 0, :], -1.0, dtx[:, 0, :], ALU.mult, ALU.min).then_inc(su["dt_neg"], 1)
                dve.wait_ge(su["high"], 3)
                dve.tensor_tensor(xfL[:, :], xf[:, :], f32(xfH[:, :]), ALU.subtract).then_inc(su["low"], 1)
                log1p()
                dve.scalar_tensor_tensor(sc[:, :, 1, :], dtx[:, 0, :].rearrange("p (b c) -> p b c", b=NB), 0.0,
                                         dtx[:, 1, :].rearrange("p (b c) -> p b c", b=NB),
                                         ALU.max, ALU.add).then_inc(su["dt"], 1)
                dve.wait_ge(su["dt"], 1)
                dve.wait_ge(su["aexp"], 1)
                for b in range(NB):
                    i = dve.scalar_tensor_tensor(
                        dta[:, b * NT * NH:(b + 1) * NT * NH].rearrange("p (t h) -> p t h", h=NH),
                        sc[:, b, 1, :].rearrange("p (t h) -> p t h", h=NH), -1.0, over(aexp[:, :], NT),
                        ALU.mult, ALU.mult)
                i.then_inc(su["dta"], 1)
                dve.wait_ge(su["dta"], 1)
                dve.tensor_scalar(dta[:, :], dta[:, :], UNDERFLOW, None, ALU.max).then_inc(su["dta"], 1)
                dve.wait_ge(su["cs_p"], 1)
                dve.tensor_copy(sc[:, :, 0, :], F[1][:, 0:NB * NT * NH].rearrange("p (b c) -> p b c", b=NB)).then_inc(su["cs"], 1)
                dve.wait_ge(su["cs"], 1)
                dve.wait_ge(su["end_p"], 1)
                dve.tensor_tensor(sc[:, :, 2, :], F[2][:, 0:NB * NT * NH].rearrange("p (b c) -> p b c", b=NB),
                                  sc[:, :, 0, :], ALU.subtract).then_inc(su["end_d"], 1)
                dve.wait_ge(su["end_exp"], 1)
                dve.tensor_tensor(sc[:, :, 2, :], sc[:, :, 2, :], sc[:, :, 1, :], ALU.mult).then_inc(su["end_w"], 1)
                dve.wait_ge(su["high"], 6)
                dve.tensor_tensor(cxL, cx, f32(cxH), ALU.subtract).then_inc(su["low"], 1)
                dve.tensor_tensor(wkL, wqk[:, 1, :], f32(wkH), ALU.subtract).then_inc(su["low"], 1)
                dve.tensor_tensor(wqL[:, :], wqk[:, 0, :], f32(wqH[:, :]), ALU.subtract).then_inc(su["low"], 1)
                for g in range(G):
                    dve.wait_ge(su["key32"], g + 1)
                    if g:
                        dve.wait_ge(su["key_in"], g)
                    dve.tensor_copy(kH, k32).then_inc(su["keyH"], 1)
                    dve.wait_ge(su["keyH"], g + 1)
                    dve.scalar_tensor_tensor(kst0, f32(kH), con[:, MK:MK + 1], k32,
                                             ALU.mult, ALU.add).then_inc(su["keyS"], 1)
                    dve.wait_ge(su["keyS"], g + 1)
                    dve.tensor_scalar(kc[:, :, g, :], kst0.rearrange("p (b s) -> p b s", b=NB),
                                      con[:, KEEP:KEEP + 1], None, ALU.mult).then_inc(su["key_in"], 1)
                dve.wait_ge(su["val_p"], 1)
                dve.tensor_copy(vc[:, :, :], M[0][0:S, :].rearrange("p (b d) -> p b d", b=NB)).then_inc(su["val_in"], 1)

            def unit(m, u):
                a, k = M[2 * u % 3], M[(2 * u + 1) % 3]
                reach(dve, "tanh_m", m, u + 1)
                dve.scalar_tensor_tensor(mt_u[:, u % 2, :], mt_u[:, u % 2, :], 1.0, a[:, :],
                                         ALU.add, ALU.mult).then_inc(done["moe_u"], 1)
                reach(dve, "moe_u", m, u + 1)
                reach(dve, "ab", m, 2 * u + 2)
                reach(dve, "moe_h", m, u - 1)
                dve.tensor_tensor(mt_h[:, u % 2, :], mt_u[:, u % 2, :], k[:, :], ALU.mult).then_inc(done["moe_h0"], 1)

            def units(m, which):
                if m is not None:
                    for u in which:
                        unit(m, u)

            def statistics(k, b):
                reach(dve, f"res{k}", b, 1)
                for t in range(NT):
                    dve.bn_stats(bst[:, k, t, :], res[k][:, t, :]).then_inc(done[f"stat{k}"], 1)
                for t in range(NT):
                    reach(dve, f"stat{k}", b, t + 1, alone=True)
                    dve.bn_aggr(mv[:, k, t, :], bst[:, k, t, :]).then_inc(done[f"mv{k}"], 1)

            def normalise(k, b, out):
                reach(dve, f"mv{k}", b, NT)
                reach(dve, f"rstd{k}", b, 1)
                for t in range(NT):
                    dve.tensor_scalar(out[:, t, :], res[k][:, t, :], mv[:, k, t, 0:1], rstd[:, k, 1, t:t + 1],
                                      ALU.subtract, ALU.mult).then_inc(done[f"norm{k}"], 1)

            def experts_end(m):
                reach(dve, "yT", m, 1)
                reach(dve, "kept", m, 1)
                dve.tensor_tensor(res[2][:, :, :], M[0][:, :].rearrange("p (t d) -> p t d", t=NT),
                                  x2[:, m, :, :], ALU.add).then_inc(done["res2"], 1)
                statistics(2, m)
                normalise(2, m, x2[:, m, :, :])

            def front(b, m):
                for s, k in enumerate((2, 1, 0)):
                    for i in range(NC):
                        if s == 0:
                            reach(dve, "tap0", b, i + 1)
                        else:
                            reach(dve, "conv", b, NC * (s - 1) + i + 1)
                        dve.scalar_tensor_tensor(acc[:, i, :], raw[:, i, k:k + L], cwh[:, TAPS * i + k:TAPS * i + k + 1],
                                                 acc[:, i, :], ALU.mult, ALU.add).then_inc(done["conv"], 1)
                for h in range(NH):
                    reach(dve, "tanh_z", b, h + 1)
                    dve.scalar_tensor_tensor(gz[:, h, :], gz[:, h, :], 1.0, F[(3, 0)[h]][:, :],
                                             ALU.add, ALU.mult).then_inc(done["gz_r"], 1)
                reach(dve, "copies", b, 1)
                for h in range(NH):
                    reach(dve, "csb", b, h + 1)
                    reach(dve, "ecs_r", b, h + 1)
                    for c in range(NT):
                        dve.tensor_scalar(dd[:, h, c * P:(c + 1) * P], F[1 + h][:, c * P:(c + 1) * P],
                                          scb[:, 0, NH * c + h:NH * c + h + 1], 0.0,
                                          ALU.subtract, ALU.min).then_inc(done["dd_r"], 1)
                if not isinstance(b, int):
                    dve.wait_ge(c_low, 16 * b)
                for i in range(NC):
                    reach(dve, "tanh_c", b, i + 1)
                    dve.scalar_tensor_tensor(xs[:, i, :], xs[:, i, :], 1.0, acc[:, i, :],
                                             ALU.add, ALU.mult).then_inc(done["xs_r"], 1)
                units(m, AT_CONV)
                reach(dve, "btT", b, 1)
                for h in range(NH):
                    for c in range(NT - 1):
                        dve.tensor_scalar(bw[:, h, c, :], F[1][:, c * NS:(c + 1) * NS],
                                          scb[:, 2, NH * c + h:NH * c + h + 1], None, ALU.mult).then_inc(done["bw_r"], 1)
                reach(dve, "gdot", b, 1)
                dve.tensor_tensor(gm[:, :].rearrange("p (c q) -> p c q", c=NT),
                                  F[2][:, :].rearrange("p (c q) -> p c q", c=NT), over(tri, NT),
                                  ALU.mult).then_inc(done["gm_r"], 1)
                units(m, AT_SCAN)
                reach(dve, "gm_r", b, 1)
                for h in range(NH):
                    reach(dve, "dec", b, h + 1)
                    for c in range(NT):
                        q = slice(c * P, (c + 1) * P)
                        dve.scalar_tensor_tensor(dd[:, h, q], dd[:, h, q], scb[:, 1, NH * c + h:NH * c + h + 1],
                                                 gm[:, q], ALU.mult, ALU.mult).then_inc(done["m_r"], 1)
                for c in range(NT - 1):
                    for h in range(NH):
                        new = F[(1, 3)[h]][0:NS, c * P:(c + 1) * P]
                        if c == 0:
                            reach(dve, "upd", b, h + 1)
                            i = dve.tensor_copy(st[:, h, 0, :], new)
                        else:
                            reach(dve, "s_r", b, NH * (c - 1) + h + 1)
                            i = dve.scalar_tensor_tensor(st[:, h, c, :], st[:, h, c - 1, :],
                                                         scb[0:NS, 3, NH * c + h:NH * c + h + 1], new,
                                                         ALU.mult, ALU.add)
                        i.then_inc(done["s_r"], 1)
                for h in range(NH):
                    reach(dve, "ydot", b, h + 1)
                    dve.scalar_tensor_tensor(y1[:, h, :], xs[:, h, :], sm[:, DSK + h:DSK + h + 1],
                                             F[(0, 2)[h]][:, :], ALU.mult, ALU.add).then_inc(done["y1_r"], 1)
                reach(dve, "wout_d", b, 1)
                dve.wait_ge(ld_tok, 16 * (b + 1))
                dve.tensor_tensor(res[0][:, :, :], F[1][:, :].rearrange("p (t d) -> p t d", t=NT),
                                  xt[:, :, :], ALU.add).then_inc(done["res0"], 1)
                statistics(0, b)
                units(m, AT_NORM1)
                normalise(0, b, x1)
                reach(dve, "x1h", b, 1)
                dve.tensor_tensor(x1L[:, :], F[3][:, :], f32(x1H[:, :]), ALU.subtract).then_inc(done["x1l"], 1)
                for g in range(G):
                    reach(dve, "q32_r", b, g + 1)
                    dve.tensor_copy(qst[:, g, :], q32[:, g % 2, :]).then_inc(done["qh_r"], 1)
                    reach(dve, "qh_r", b, g + 1)
                    dve.scalar_tensor_tensor(qst[:, g, :], f32(qst[:, g, :]), con[:, MQ:MQ + 1], q32[:, g % 2, :],
                                             ALU.mult, ALU.add).then_inc(done["qst_r"], 1)
                for i in range(NT * G):
                    t, g = divmod(i, G)
                    reach(dve, "tsc", b, i + 1)
                    dve.tensor_reduce(smax[:, t, J * g:J * g + J], F[g][:, 0:J * S].rearrange("p (j s) -> p j s", j=J),
                                      AX.X, ALU.max).then_inc(done["tmax"], 1)
                reach(dve, "tmax", b, NT * G)
                dve.tensor_copy(smH[:, :, :], smax[:, :, :]).then_inc(done["msplit"], 1)
                reach(dve, "msplit", b, 1)
                dve.tensor_copy(smHL[:, :, 0, :], f32(smH[:, :, :])).then_inc(done["msplit"], 1)
                dve.tensor_tensor(smHL[:, :, 1, :], smax[:, :, :], f32(smH[:, :, :]), ALU.subtract).then_inc(done["msplit"], 1)
                units(m, AT_MAX)
                units(m, AT_SCORE)
                reach(dve, "pv", b, G)
                dve.reciprocal(rsum[:, :], F[3][:, :]).then_inc(done["rs_r"], 1)
                reach(dve, "rs_r", b, 1)
                dve.tensor_tensor(att[:, :], F[2][:, :], rsum[:, :], ALU.mult).then_inc(done["att_r"], 1)
                reach(dve, "wo_d", b, 1)
                reach(dve, "bo_r", b, 1)
                reach(dve, "kept", b - 1, 1)
                dve.tensor_tensor(res[1][:, :, :], F[0][:, :].rearrange("p (t d) -> p t d", t=NT),
                                  x1bo[:, :, :], ALU.add).then_inc(done["res1"], 1)
                statistics(1, b)
                units(m, AT_NORM2)
                normalise(1, b, res[1])
                reach(dve, "x2h", b, 1)
                dve.tensor_tensor(x2L[:, :], F[1][:, :], f32(x2H[:, :]), ALU.subtract).then_inc(done["x2l"], 1)
                if m is not None:
                    experts_end(m)
                router(b)

            def router(b):
                def per_expert(ap):
                    return ap.unsqueeze(2).broadcast_to([P, NT, E])

                logits = F[0][:, 0:NT * E].rearrange("p (t e) -> p t e", t=NT)
                step = [0]

                def then(i, alone=False):
                    i.then_inc(done["lgv"], 1)
                    step[0] += 1
                    reach(dve, "lgv", b, step[0], alone)

                reach(dve, "logit", b, 1)
                then(dve.tensor_reduce(lmx[:, 0, :], logits, AX.X, ALU.max))
                then(dve.tensor_tensor(lg[:, 0, :, :], logits, per_expert(lmx[:, 0, :]), ALU.subtract))
                reach(dve, "lexp", b, 1)
                then(dve.tensor_reduce(lmx[:, 1, :], lg[:, 1, :, :], AX.X, ALU.add))
                then(dve.reciprocal(lmx[:, 2, :], lmx[:, 1, :]))
                then(dve.tensor_tensor(lg[:, 2, :, :], lg[:, 1, :, :], per_expert(lmx[:, 2, :]), ALU.mult), alone=True)
                for t in range(NT):
                    dve.max(top[:, t, :], lg[:, 2, t, :]).then_inc(done["topv"], 1)
                for t in range(NT):
                    reach(dve, "topv", b, t + 1, alone=True)
                    dve.max_index(topi[:, t, :], top[:, t, :], lg[:, 2, t, :]).then_inc(done["topv"], 1)
                reach(dve, "topv", b, 2 * NT)
                then(dve.tensor_copy(topf[:, :, :], topi[:, :, :]))
                then(dve.tensor_tensor(lmx[:, 1, :], top[:, :, 0], top[:, :, 1], ALU.add))
                then(dve.reciprocal(lmx[:, 3, :], lmx[:, 1, :]))
                iota = con[:, IOTA:IOTA + E]
                for t in range(NT):
                    dve.tensor_scalar(lg[:, 3, t, :], iota, topf[:, t, 0:1], None, ALU.is_equal).then_inc(done["topv"], 1)
                for t in range(NT):
                    reach(dve, "topv", b, 2 * NT + t + 1)
                    dve.scalar_tensor_tensor(lg[:, 3, t, :], iota, topf[:, t, 1:2], lg[:, 3, t, :],
                                             ALU.is_equal, ALU.add).then_inc(done["topv"], 1)
                reach(dve, "topv", b, 4 * NT)
                then(dve.tensor_tensor(lg[:, 4, :, :], lg[:, 2, :, :], lg[:, 3, :, :], ALU.mult))
                then(dve.tensor_tensor(lg[:, 5, :, :], lg[:, 4, :, :], per_expert(lmx[:, 3, :]), ALU.mult))
                then(dve.tensor_copy(cH[:, :, :], lg[:, 5, :, :]))
                then(dve.tensor_copy(cHL[:, :, 0, :], f32(cH[:, :, :])))
                then(dve.tensor_tensor(cHL[:, :, 1, :], lg[:, 5, :, :], f32(cH[:, :, :]), ALU.subtract))

            setup()
            front(0, None)
            with dve.Fori(1, NB) as b:
                front(b, b - 1)
            for u in range(U):
                unit(NB - 1, u)
            experts_end(NB - 1)

        @block.gpsimd
        def _(pool):
            def setup():
                pool.memset(half[:, :], -0.5).then_inc(su["half"], 1)
                pool.memset(raw[:, :, 0:TAPS - 1], 0.0).then_inc(su["zero"], 1)
                pool.memset(kst[:, :, :].bitcast(F32), 0.0).then_inc(su["zero"], 1)
                pool.memset(vst[:, :, :], 0.0).then_inc(su["zero"], 1)
                pool.memset(mt[:, :].bitcast(F32), 0.0).then_inc(su["zero"], 1)
                pool.memset(ct[:, :].bitcast(F32), 0.0).then_inc(su["zero"], 1)
                pool.wait_ge(su["zero"], 5)
                pool.memset(pr[64:P, :, :, :], 0.0).then_inc(su["zero"], 1)
                pool.wait_ge(su["zero"], 6)
                pool.wait_ge(ld_c, 32)
                pool.tensor_copy(sel[:, :], con[:, IND:IND + HA + E]).then_inc(su["sel"], 1)

            def setup_experts():
                pool.wait_ge(su["moeH"], 1)
                pool.tensor_scalar(w1s[:, 0, :], w1s[:, 0, :], 0.5, None, ALU.mult).then_inc(su["half"], 1)
                pool.wait_ge(su["half"], 2)
                pool.tensor_tensor(w1L[:, 0, :], w1s[:, 0, :], w1H[:, 0, :].bitcast(F32), ALU.subtract).then_inc(su["moeL"], 1)
                pool.wait_ge(su["moeH"], 2)
                pool.tensor_tensor(w1L[:, 1, :], w1s[:, 1, :], w1H[:, 1, :].bitcast(F32), ALU.subtract).then_inc(su["moeL"], 1)

            def unit(m, u):
                reach(pool, "moe_h0", m, u + 1)
                reach(pool, "cbs", m, u // FC + 1)
                reach(pool, "w2d", m, u - 1)
                pool.tensor_tensor(mt_h[:, u % 2, :], mt_h[:, u % 2, :], cb[:, u // FC, :], ALU.mult).then_inc(done["moe_h"], 1)

            def units(m, which):
                if m is not None:
                    for u in which:
                        unit(m, u)

            def deviation(k, b):
                reach(pool, f"mv{k}", b, NT, alone=True)
                pool.tensor_scalar(rstd[:, k, 0, :], mv[:, k, :, 1], EPS, None, ALU.add).then_inc(done[f"eps{k}"], 1)
                reach(pool, f"eps{k}", b, 1)
                pool.tensor_tensor(rstd[:, k, 1, :], rstd[:, k, 0, :], half[:, :], ALU.pow).then_inc(done[f"rstd{k}"], 1)

            def front(b, m):
                reach(pool, "wo_d", b - 1, 1)
                pool.tensor_copy(scb[:, :, :], sc[:, b, :, :]).then_inc(done["copies"], 1)
                if isinstance(b, int):
                    pool.wait_ge(su["key_in"], G)
                    pool.wait_ge(su["val_in"], 1)
                    pool.wait_ge(su["zero"], 3)
                for j in range(J):
                    reach(pool, "copies", b, j + 1)
                    rows = slice(32 * j, 32 * j + 32)
                    pool.tensor_copy(kst[rows, j:HA:J, :], kc[rows, b, :, :]).then_inc(done["copies"], 1)
                reach(pool, "copies", b, J + 1)
                for g in range(G):
                    pool.tensor_copy(vst[0:S, J * g:J * g + J, DH * g:DH * g + DH],
                                     vc[:, b, 32 * g:32 * g + 32].rearrange("p (j d) -> p j d", j=J)).then_inc(done["copies"], 1)
                units(m, AT_CONV)
                pool.wait_ge(c_low, 16 * (b + 1))
                for h in range(NH):
                    reach(pool, "ecs_r", b, h + 1)
                    pool.tensor_tensor(ecs[:, h, :], clow[:, :], ecs[:, h, :], ALU.mult).then_inc(done["csd_r"], 1)
                units(m, AT_SCAN)
                for h in range(NH):
                    reach(pool, "y1_r", b, h + 1)
                    pool.tensor_tensor(y1[:, h, :], y1[:, h, :], gz[:, h, :], ALU.mult).then_inc(done["yg_r"], 1)
                deviation(0, b)
                units(m, AT_NORM1)
                reach(pool, "norm0", b, NT)
                pool.tensor_tensor(x1bo[:, :, :], x1[:, :, :], bo[:, :].unsqueeze(1).broadcast_to([P, NT, D]),
                                   ALU.add).then_inc(done["bo_r"], 1)
                units(m, AT_MAX)
                units(m, AT_SCORE)
                deviation(1, b)
                units(m, AT_NORM2)
                reach(pool, "norm1", b, NT)
                pool.tensor_copy(x2[:, b, :, :], res[1][:, :, :]).then_inc(done["kept"], 1)
                if m is not None:
                    deviation(2, m)

            setup()
            pool.wait_ge(su["end_w"], 1)
            pool.wait_ge(su["total"], 1)
            pool.wait_ge(ld_late, 64)
            setup_experts()
            front(0, None)
            with pool.Fori(1, NB) as b:
                front(b, b - 1)
            for u in range(U):
                unit(NB - 1, u)
            deviation(2, NB - 1)


def kernel(**inputs):
    import concourse.bacc as bacc
    from concourse.bass_utils import run_bass_kernel_spmd

    a = {k: np.asarray(v) for k, v in inputs.items()}
    heads = np.arange(HA).reshape(G, J)
    stacked = (heads[:, :, None] * DH + (np.arange(32) % DH)[None, None, :]).reshape(-1)
    packed = (heads.T[:, :, None] * DH + np.arange(DH)[None, None, :]).reshape(-1)
    x = a["x"].reshape(NB * L, D)
    small = np.concatenate([
        a["L0_attn_conv_w"].reshape(NC, P, TAPS).transpose(1, 0, 2).reshape(P, NC * TAPS),
        a["L0_attn_conv_b"].reshape(NC, P).T,
        np.broadcast_to(a["L0_attn_A_log"], (P, NH)),
        np.broadcast_to(a["L0_attn_dt_bias"], (P, NH)),
        np.broadcast_to(a["L0_attn_D_skip"], (P, NH)),
        a["L0_xattn_bq"][stacked].reshape(G, P).T,
        a["L0_xattn_bk"][stacked].reshape(G, P).T,
        a["L0_xattn_bv"][packed].reshape(P, 1),
    ], axis=1)
    arrays = {
        "x_feat": x.T,
        "x_tok": x.reshape(NB, NT, P, D).transpose(2, 0, 1, 3),
        "ctx_feat": a["ctx_1024"].reshape(NB * S, D).T,
        "small": small,
        "cst": constants(),
        "bo_row": np.broadcast_to(a["L0_xattn_bo"], (P, D)),
        "w_in": a["L0_attn_W_in"].T,
        "w_out": a["L0_attn_W_out"].T.reshape(NH, P, D).transpose(1, 0, 2),
        "wq": a["L0_xattn_Wq"].T[:, stacked],
        "wk": a["L0_xattn_Wk"].T[:, stacked],
        "wv": a["L0_xattn_Wv"].T,
        "wo": a["L0_xattn_Wo"].T[packed, :],
        "router": a["L0_ffn_router_w"].T,
        "w1": a["L0_ffn_w1"].transpose(2, 0, 1).reshape(D, E * FC * P),
        "v1": a["L0_ffn_v1"].transpose(2, 0, 1).reshape(D, E * FC * P),
        "w2": a["L0_ffn_w2"].reshape(E * FC, P, D).transpose(1, 0, 2),
    }
    arrays = {k: np.ascontiguousarray(v) for k, v in arrays.items()}
    nc = bacc.Bacc("TRN2", target_bir_lowering=False, num_devices=1)
    args = {k: nc.dram_tensor(k, v.shape, mybir.dt.from_np(v.dtype), kind="ExternalInput").ap()
            for k, v in arrays.items()}
    out = nc.dram_tensor("out", (P, NB, NT, D), F32, kind="ExternalOutput").ap()
    decoder_kernel(nc, **args, out=out)
    r = run_bass_kernel_spmd(nc, [arrays], core_ids=[0])
    return r.results[0]["out"].transpose(1, 2, 0, 3).reshape(NB, L, D)
```

```python
from contextlib import ExitStack

import numpy as np
import concourse.bass as bass
from concourse import mybir

F32 = mybir.dt.float32
F32R = mybir.dt.float32r
U32 = mybir.dt.uint32
ALU = mybir.AluOpType
ACT = mybir.ActivationFunctionType
AX = mybir.AxisListType

P = 128
NB, L, D = 4, 512, 128
NT = L // P
NS = 64
NC = 3
TAPS = 4
NH = 2
HA, DH, G, J = 16, 8, 4, 4
S = 77
E, FC = 8, 2
U = E * FC
EPS = 1e-5
UNDERFLOW = -110.0
LOG_TERMS = 8
SCALE = float(DH) ** -0.5
CW, CB, ALOG, DTB, DSK, BQ, BK, BV = 0, 12, 15, 17, 19, 21, 25, 29
NSMALL = 30
IDENT, TRI, LAST, ONES, MQ, MK, KEEP, IND, SELC, IOTA = 0, 128, 256, 384, 512, 513, 514, 515, 531, 539
NCST = 547
WZ, WX, WDT = 0, 256, 640


def constants():
    c = np.zeros((P, NCST), np.float32)
    p = np.arange(P)
    c[:, IDENT:IDENT + P] = np.eye(P)
    c[:, TRI:TRI + P] = p[:, None] <= p[None, :]
    c[P - 1, LAST:LAST + P] = 1.0
    for g in range(G):
        c[:S, ONES + 32 * g + 8 * g:ONES + 32 * g + 8 * g + 8] = 1.0
    r = p % 32
    c[:, MQ] = -1.0 * ((r >= 8) & (r < 16))
    c[:, MK] = -1.0 * ((r >= 16) & (r < 24))
    c[:, KEEP] = r < 24
    for h in range(HA):
        c[h, IND + h] = c[HA + h, IND + h] = -1.0
    for e in range(E):
        c[e, SELC + e] = c[E + e, SELC + e] = 1.0
    c[:, IOTA:IOTA + E] = np.arange(E)
    return c


def decoder_kernel(nc, x_feat, x_tok, ctx_feat, small, cst, bo_row, w_in, w_out, wq, wk, wv, wo,
                   router, w1, v1, w2, out):
    with ExitStack() as ctx:
        def sb(name, shape, dt=F32):
            return ctx.enter_context(nc.sbuf_tensor(name, shape, dt))

        def sem(name):
            return ctx.enter_context(nc.semaphore(name))

        xf = sb("xf", [P, NB * L])
        xfH = sb("xfH", [P, NB * L], F32R)
        xfL = sb("xfL", [P, NB * L], F32R)
        sm = sb("sm", [P, NSMALL])
        con = sb("con", [P, NCST])
        bo = sb("bo", [P, D])
        winH = sb("winH", [P, 640], F32R)
        winL = sb("winL", [P, 640], F32R)
        wout = sb("wout", [P, NH, D])
        wqH = sb("wqH", [P, G * P], F32R)
        wqL = sb("wqL", [P, G * P], F32R)
        wvs = sb("wvs", [P, D])
        wos = sb("wos", [P, D])
        wr = sb("wr", [P, E])
        w1H = sb("w1H", [P, 2, E * FC * P], F32R)
        w1L = sb("w1L", [P, 2, E * FC * P], F32R)
        w2s = sb("w2s", [P, E * FC, D])
        ident = con[:, IDENT:IDENT + P]
        tri = con[:, TRI:TRI + P]
        last = con[:, LAST:LAST + P]
        ones = con[:, ONES:ONES + P]
        cwh = sb("cwh", [P, NC * TAPS + NC])
        sel = sb("sel", [P, HA + E], F32R)
        aexp = sb("aexp", [P, NH])
        dtx = sb("dtx", [P, 5, NB * NT * NH])
        dta = sb("dta", [P, NB * NT * NH])
        sc = sb("sc", [P, NB, 4, NT * NH])
        kc = sb("kc", [P, NB, G, S], F32R)
        vc = sb("vc", [S, NB, D])
        half = sb("half", [P, NT])
        kst = sb("kst", [P, HA, S], F32R)
        vst = sb("vst", [P, HA, 32])
        scb = sb("scb", [P, 4, NT * NH])
        xt = sb("xt", [P, NT, D])
        raw = sb("raw", [P, NC, TAPS - 1 + L])
        acc = sb("acc", [P, NC, L])
        xs = sb("xs", [P, NC, L])
        gz = sb("gz", [P, NH, L])
        dd = sb("dd", [P, NH, L])
        bw = sb("bw", [P, NH, NT - 1, NS])
        st = sb("st", [NS, NH, NT - 1, D])
        res = [sb(f"res{k}", [P, NT, D]) for k in range(3)]
        bst = sb("bst", [P, 3, NT, 6])
        mv = sb("mv", [P, 3, NT, 2])
        rstd = sb("rstd", [P, 3, 2, NT])
        x1 = sb("x1", [P, NT, D])
        x1H = sb("x1H", [P, L], F32R)
        x1L = sb("x1L", [P, L], F32R)
        qst = sb("qst", [P, G, L], F32R)
        smax = sb("smax", [P, NT, HA])
        smH = sb("smH", [P, NT, HA], F32R)
        smHL = sb("smHL", [P, NT, 2, HA])
        mt = sb("mt", [P, L], F32R)
        pr = sb("pr", [P, 2, J, L])
        rsum = sb("rsum", [P, L])
        att = sb("att", [P, L])
        x2H = sb("x2H", [P, L], F32R)
        x2L = sb("x2L", [P, L], F32R)
        lg = sb("lg", [P, 6, NT, E])
        lmx = sb("lmx", [P, 4, NT])
        top = sb("top", [P, NT, 8])
        topi = sb("topi", [P, NT, 8], U32)
        topf = sb("topf", [P, NT, 8])
        stage = sb("stage", [P, 8, L])
        mt_u, mt_h, ye = stage[:, 0:2, :], stage[:, 2:5, :], stage[:, 5:7, :]
        win = gz[:, :, :].rearrange("p h l -> p (h l)")[:, 0:642]
        wqk = dd
        wkH, wkL, cxH, cxL = qst[:, 0, :], qst[:, 1, :], qst[:, 2, 0:NB * S], qst[:, 3, 0:NB * S]
        cx = att[:, 0:NB * S]
        k32 = x1[:, :, :].rearrange("p t d -> p (t d)")[:, 0:NB * S]
        kst0 = res[1][:, :, :].rearrange("p t d -> p (t d)")[:, 0:NB * S]
        kH = x1H[:, 0:NB * S]
        w1s = stage[:, :, :].rearrange("p e l -> p (e l)").rearrange("p (w k) -> p w k", w=2)
        y1 = acc
        ecs = pr[0:NS, 0, 0:NH, :]
        clow = pr[0:NS, 0, NH, :]
        gm = x2c = rsum
        q32 = dd
        x1bo = res[0]

        def xtok(h, c):
            return raw[:, h, TAPS - 1 + c * P:TAPS - 1 + (c + 1) * P]

        F = [ctx.enter_context(nc.psum_tensor(f"front{i}", [P, 512], F32)) for i in range(4)]
        M = [ctx.enter_context(nc.psum_tensor(f"moe{i}", [P, 512], F32)) for i in range(3)]
        Y = ctx.enter_context(nc.psum_tensor("moe_y", [P, 512], F32))
        KB = (M[0], M[1], M[2], Y)

        ld_x0, ld_x, ld_tok, ld_late, ld_ctx, ld_w, ld_c, ld_moe = (sem(n) for n in (
            "ld_x0", "ld_x", "ld_tok", "ld_late", "ld_ctx", "ld_w", "ld_c", "ld_moe"))
        c_low, stored = sem("c_low"), sem("stored")
        su = {n: sem(f"su_{n}") for n in (
            "high", "low", "taps", "dt_p", "dt_x", "dt_neg", "dt_exp", "log1p", "dt", "dta", "aexp",
            "cs_p", "cs", "end_p", "end_d", "end_exp", "total", "key_p", "key32", "keyH",
            "keyS", "key_in", "val_p", "val_in", "zero", "sel", "moeH", "moeL", "moeLv", "half")}

        counts = dict(
            proj=5, csb=2, xtT=2, btT=1, gdot=1, upd=2, ydot=2, wout_d=1, x1T=1, qdot=4, tsc=16,
            mT=1, ksc=HA, pv=4, wo_d=1, x2T=1, logit=1, ab=2 * U, w2d=U,
            raw_c=3, tap0=3, tanh_c=3, tanh_z=2, ecs_r=2, dd_r=8, dec=2, xtok_r=2, x1h=1, q32_r=4, mt_r=1,
            prob=HA, attb_r=1, x2h=1, x2c_r=1, lexp=1, tanh_m=U, ye_r=E,
            conv=9, xs_r=3, gz_r=2, bw_r=6, gm_r=1, m_r=2, s_r=6, y1_r=2,
            res0=1, res1=1, stat0=4, stat1=4, stat2=4, mv0=4, mv1=4, mv2=4,
            norm0=4, norm1=4, norm2=4, x1l=1, qh_r=4, qst_r=4, tmax=16, msplit=3,
            att_r=1, rs_r=1, x2l=1, lgv=10, topv=16, moe_u=U, moe_h=U,
            scb_r=1, copies=8, csd_r=2, yg_r=2, bo_r=1, eps0=1, eps1=1, eps2=1, rstd0=1, rstd1=1, rstd2=1,
            yadd=E,
        )
        done = {n: sem(n) for n in counts}

        def reach(eng, name, b, k, alone=False):
            if k <= 0:
                return
            v = counts[name] * b + k
            if not isinstance(v, int):
                if alone:
                    v = eng.to_reg(v)
                    eng.wait_ge(ld_c, 32)
                eng.wait_ge(done[name], v)
            elif v > 0:
                eng.wait_ge(done[name], v)

        def row(b):
            return bass.ds(b * L, L)

        block = ctx.enter_context(nc.Block())
        LAST_TAP = (2, 0, 1)

        AT_CONV, AT_SCAN, AT_GATE, AT_NORM, AT_QUERY, AT_MAX, AT_SCORE = (
            range(0, 3), range(3, 5), range(5, 6), range(6, 8), range(8, 9), range(9, 11), range(11, 16))

        def at_score(g):
            return AT_SCORE[2 * g:2 * g + 2] if g < 2 else AT_SCORE[g + 2:g + 3]

        @block.sync
        def _(sp):
            sp.dma_start(win, w_in).then_inc(ld_w, 16)
            sp.dma_start(xf[:, 0:L], x_feat[:, 0:L]).then_inc(ld_x0, 16)
            sp.dma_start(con[:, :], cst).then_inc(ld_c, 16)
            sp.dma_start(sm[:, :], small).then_inc(ld_c, 16)
            sp.dma_start(xf[:, L:], x_feat[:, L:]).then_inc(ld_x, 16)
            sp.dma_start(cx, ctx_feat).then_inc(ld_ctx, 16)
            sp.dma_start(wqk[:, 1, :], wk).then_inc(ld_ctx, 16)
            sp.dma_start(wqk[:, 0, :], wq).then_inc(ld_ctx, 16)
            sp.dma_start(wvs[:, :], wv).then_inc(ld_ctx, 16)
            sp.dma_start(wout[:, :, :], w_out).then_inc(ld_late, 16)
            sp.dma_start(bo[:, :], bo_row).then_inc(ld_late, 16)
            sp.dma_start(wos[:, :], wo).then_inc(ld_late, 16)
            sp.dma_start(wr[:, :], router).then_inc(ld_late, 16)
            sp.dma_start(w1s[:, 0, :], w1).then_inc(ld_moe, 16)
            sp.dma_start(w1s[:, 1, :], v1).then_inc(ld_moe, 16)
            sp.dma_start(w2s[:, :, :], w2).then_inc(ld_moe, 16)

            def load_tokens(b):
                reach(sp, "res0", b - 1, 1)
                sp.dma_start(xt[:, :, :], x_tok[:, b, :, :]).then_inc(ld_tok, 16)

            def lower_c(b):
                reach(sp, "csd_r", b - 1, 2)
                reach(sp, "gdot", b - 1, 1)
                reach(sp, "xs_r", b, 1)
                sp.dma_start(clow[:, :], xs[NS:P, 2, :]).then_inc(c_low, 16)

            def store(b):
                reach(sp, "norm2", b, 4)
                sp.dma_start(out[:, b, :, :], res[2][:, :, :]).then_inc(stored, 16)

            load_tokens(0)
            lower_c(0)
            with sp.Fori(1, NB) as b:
                load_tokens(b)
                lower_c(b)
                store(b - 1)
                total = sp.to_reg(16 * b)
                sp.wait_ge(ld_c, 32)
                sp.wait_ge(stored, total)
            store(NB - 1)
            sp.wait_ge(stored, 16 * NB)

        @block.tensor
        def _(pe):
            def split3(o, wH, wL, xH, xL, signal):
                pe.matmul(o, wH, xH, start=True, stop=False)
                pe.matmul(o, wH, xL, start=False, stop=False)
                pe.matmul(o, wL, xH, start=False, stop=True).then_inc(signal, 1)

            def steps():
                pe.wait_ge(ld_x, 16)
                for t in range(NB * NT):
                    mm = pe.matmul(M[0][:, NH * t:NH * t + NH], xf[:, t * P:(t + 1) * P],
                                   win[:, WDT:WDT + NH], start=True, stop=True)
                mm.then_inc(su["dt_p"], 1)

            def sums():
                pe.wait_ge(ld_c, 32)
                pe.wait_ge(su["dta"], 2)
                pe.matmul(M[1][:, 0:NB * NT * NH], tri, dta[:, :], start=True, stop=True).then_inc(su["cs_p"], 1)
                pe.wait_ge(su["cs"], 1)
                pe.matmul(M[2][:, 0:NB * NT * NH].rearrange("p (b c) -> p b c", b=NB), last,
                          sc[:, :, 0, :], start=True, stop=True).then_inc(su["end_p"], 1)

            def keys():
                pe.wait_ge(su["high"], 6)
                pe.wait_ge(su["low"], 6)
                pe.wait_ge(su["end_d"], 1)
                pe.wait_ge(su["total"], 1)
                for g in range(G):
                    split3(KB[g][:, 0:NB * S], wkH[:, g * P:(g + 1) * P], wkL[:, g * P:(g + 1) * P],
                           cxH, cxL, su["key_p"])

            def values_in():
                pe.wait_ge(su["key32"], G)
                for b in range(NB):
                    mm = pe.matmul(M[0][0:S, b * D:(b + 1) * D], cx[:, b * S:(b + 1) * S], wvs[:, :],
                                   start=True, stop=True)
                mm.then_inc(su["val_p"], 1)

            def unit(m, u):
                e, f = divmod(u, FC)
                for which in range(2):
                    k = 2 * u + which
                    if k >= 3:
                        reach(pe, "moe_u" if (k - 3) % 2 == 0 else "moe_h", m, (k - 3) // 2 + 1)
                    w = slice(u * P, (u + 1) * P)
                    split3(M[k % 3][:, :], w1H[:, which, w], w1L[:, which, w], x2H[:, :], x2L[:, :], done["ab"])
                if u >= 2:
                    down(m, u - 2)

            def down(m, u):
                if u == 0:
                    reach(pe, "lgv", m, 2)
                elif u % FC == 0:
                    reach(pe, "ye_r", m, u // FC)
                reach(pe, "moe_h", m, u + 1)
                for t in range(NT):
                    mm = pe.matmul(Y[:, t * D:(t + 1) * D], mt_h[:, u % 3, t * P:(t + 1) * P], w2s[:, u, :],
                                   start=(u % FC == 0 and t == 0), stop=(u % FC == FC - 1 and t == NT - 1))
                mm.then_inc(done["w2d"], 1)

            def logits(b):
                reach(pe, "x2c_r", b, 1)
                for t in range(NT):
                    mm = pe.matmul(Y[:, t * E:(t + 1) * E], x2c[:, t * P:(t + 1) * P], wr[:, :],
                                   start=True, stop=True)
                mm.then_inc(done["logit"], 1)
                reach(pe, "x2h", b, 1)
                reach(pe, "x2l", b, 1)

            def experts_end(m):
                down(m, U - 2)
                down(m, U - 1)

            def units(m, which):
                if m is not None:
                    for u in which:
                        unit(m, u)

            def columns(m):
                reach(pe, "norm1", m, 4)
                for t in range(NT):
                    mm = pe.transpose(F[0][:, t * P:(t + 1) * P], res[1][:, t, :], ident)
                mm.then_inc(done["x2T"], 1)

            def front(b, m):
                def project(bank, col):
                    split3(F[bank][:, :], winH[:, col:col + P], winL[:, col:col + P],
                           xfH[:, row(b)], xfL[:, row(b)], done["proj"])

                def project_z():
                    reach(pe, "tap0", b, 3)
                    project(3, WZ)
                    if m is not None:
                        logits(m)
                    project(0, WZ + P)

                for i in range(NC):
                    project(1 + i, WX + i * P)
                if m is None:
                    steps()
                    pe.wait_ge(su["zero"], 5)
                    pe.wait_ge(su["sel"], 1)
                    project_z()
                    sums()
                reach(pe, "scb_r", b, 1)
                for h in range(NH):
                    reach(pe, "tap0", b, 1 + h)
                    for c in range(NT):
                        col = scb[:, 0, NH * c + h:NH * c + h + 1]
                        mm = pe.matmul(F[1 + h][:, c * P:(c + 1) * P], col.to_broadcast([P, P]), ident,
                                       start=True, stop=True)
                    mm.then_inc(done["csb"], 1)
                if m is not None:
                    columns(m)
                    project_z()
                units(m, AT_CONV)
                for h in range(NH):
                    reach(pe, "xs_r", b, h + 2)
                    reach(pe, "gz_r", b, h + 1)
                    for c in range(NT):
                        mm = pe.transpose(F[(3, 0)[h]][:, c * P:(c + 1) * P], xs[:, h, c * P:(c + 1) * P], ident)
                    mm.then_inc(done["xtT"], 1)
                reach(pe, "dd_r", b, 4, alone=True)
                for c in range(NT - 1):
                    mm = pe.transpose(F[1][:, c * NS:(c + 1) * NS], xs[0:NS, 2, c * P:(c + 1) * P], ident[0:NS, 0:NS])
                mm.then_inc(done["btT"], 1)
                pe.wait_ge(c_low, 16 * (b + 1))
                reach(pe, "dd_r", b, 8)
                for c in range(NT):
                    mm = pe.matmul(F[2][:, c * P:(c + 1) * P], xs[0:NS, 2, c * P:(c + 1) * P],
                                   clow[:, c * P:(c + 1) * P], start=True, stop=True)
                mm.then_inc(done["gdot"], 1)
                if m is None:
                    keys()
                units(m, AT_SCAN)
                reach(pe, "bw_r", b, 6)
                reach(pe, "xtok_r", b, 2)
                for h in range(NH):
                    for c in range(NT - 1):
                        mm = pe.matmul(F[(1, 3)[h]][0:NS, c * P:(c + 1) * P], bw[:, h, c, :],
                                       xtok(h, c), start=True, stop=True)
                    mm.then_inc(done["upd"], 1)
                for h in range(NH):
                    reach(pe, "m_r", b, h + 1)
                    reach(pe, "csd_r", b, h + 1)
                    for c in range(NT):
                        o = F[(0, 2)[h]][:, c * P:(c + 1) * P]
                        mm = pe.matmul(o, xtok(h, c), dd[:, h, c * P:(c + 1) * P],
                                       start=True, stop=(c == 0))
                        if c:
                            reach(pe, "s_r", b, NH * c if c < NT - 1 else 6)
                            mm = pe.matmul(o, st[:, h, c - 1, :], ecs[:, h, c * P:(c + 1) * P],
                                           start=False, stop=True)
                    mm.then_inc(done["ydot"], 1)
                units(m, AT_GATE)
                if m is None:
                    pe.wait_ge(ld_late, 64)
                reach(pe, "yg_r", b, 2)
                for t in range(NT):
                    for h in range(NH):
                        mm = pe.matmul(F[1][:, t * D:(t + 1) * D], y1[:, h, t * P:(t + 1) * P],
                                       wout[:, h, :], start=(h == 0), stop=(h == NH - 1))
                mm.then_inc(done["wout_d"], 1)
                if m is None:
                    values_in()
                units(m, AT_NORM)
                reach(pe, "norm0", b, 4)
                for t in range(NT):
                    mm = pe.transpose(F[3][:, t * P:(t + 1) * P], x1[:, t, :], ident)
                mm.then_inc(done["x1T"], 1)
                reach(pe, "x1h", b, 1)
                reach(pe, "x1l", b, 1)
                for g in range(G):
                    split3(F[g][:, :], wqH[:, g * P:(g + 1) * P], wqL[:, g * P:(g + 1) * P],
                           x1H[:, :], x1L[:, :], done["qdot"])
                units(m, AT_QUERY)
                reach(pe, "copies", b, 4)
                for i in range(NT * G):
                    t, g = divmod(i, G)
                    if i in (8, 12):
                        units(m, AT_MAX[i // 4 - 2:i // 4 - 1])
                    if t == 0:
                        reach(pe, "qst_r", b, g + 1)
                    else:
                        reach(pe, "tmax", b, i - 3)
                    pe.matmul(F[g][:, 0:J * S], qst[:, g, t * P:(t + 1) * P],
                              kst[:, J * g:J * g + J, :].rearrange("p j s -> p (j s)"),
                              start=True, stop=True).then_inc(done["tsc"], 1)
                reach(pe, "msplit", b, 3)
                for t in range(NT):
                    mm = pe.transpose(F[0][0:2 * HA, t * P:(t + 1) * P],
                                      smHL[:, t, :, :].rearrange("p k h -> p (k h)"), ident)
                mm.then_inc(done["mT"], 1)
                reach(pe, "mt_r", b, 1)

                def scores(h):
                    i = h % 2
                    reach(pe, "prob", b, h - 1)
                    pe.matmul(F[i][0:S, :], kst[:, h, :], qst[:, h // J, :], start=True, stop=False)
                    pe.matmul(F[i][0:S, :], sel[:, h:h + 1].to_broadcast([P, S]), mt[:, :],
                              start=False, stop=True).then_inc(done["ksc"], 1)

                def values(g):
                    reach(pe, "prob", b, J * g + J)
                    if g == 0:
                        reach(pe, "copies", b, 8)
                    for o, w in ((F[2], lambda h: vst[:, h, :]), (F[3], lambda h: ones[:, 32 * g:32 * g + 32])):
                        for j in range(J):
                            mm = pe.matmul(o[32 * j:32 * j + 32, :], w(J * g + j), pr[:, g % 2, j, :],
                                           start=(g == 0), stop=(g == G - 1))
                    mm.then_inc(done["pv"], 1)

                for h in range(HA):
                    scores(h)
                    g, j = divmod(h, J)
                    if j == 1:
                        units(m, at_score(g))
                        if g:
                            values(g - 1)
                values(G - 1)
                if m is not None:
                    experts_end(m)
                reach(pe, "attb_r", b, 1)
                for t in range(NT):
                    mm = pe.matmul(F[0][:, t * D:(t + 1) * D], att[:, t * P:(t + 1) * P], wos[:, :],
                                   start=True, stop=True)
                mm.then_inc(done["wo_d"], 1)

            pe.wait_ge(ld_w, 16)
            pe.wait_ge(su["high"], 3)
            pe.wait_ge(su["low"], 3)
            front(0, None)
            pe.wait_ge(su["high"], 7)
            pe.wait_ge(su["low"], 7)
            pe.wait_ge(su["val_in"], 1)
            pe.wait_ge(su["moeH"], 2)
            pe.wait_ge(su["moeL"], 1)
            pe.wait_ge(su["moeLv"], 1)
            pe.wait_ge(ld_moe, 48)
            with pe.Fori(1, NB) as b:
                front(b, b - 1)
            columns(NB - 1)
            logits(NB - 1)
            for u in range(U):
                unit(NB - 1, u)
            experts_end(NB - 1)

        @block.scalar
        def _(act):
            def setup():
                act.wait_ge(ld_w, 16)
                act.activation(winH[:, WZ:WX], win[:, WZ:WX], ACT.Copy, scale=0.5).then_inc(su["high"], 1)
                act.activation(winH[:, WX:WDT], win[:, WX:WDT], ACT.Copy).then_inc(su["high"], 1)
                act.wait_ge(ld_x0, 16)
                act.activation(xfH[:, 0:L], xf[:, 0:L], ACT.Copy).then_inc(su["high"], 1)
                act.wait_ge(su["taps"], 1)

            def high_parts():
                act.wait_ge(ld_c, 32)
                act.activation(aexp[:, :], sm[:, ALOG:ALOG + NH], ACT.Exp).then_inc(su["aexp"], 1)
                act.wait_ge(ld_ctx, 64)
                act.activation(cxH, cx, ACT.Copy).then_inc(su["high"], 1)
                act.activation(wkH, wqk[:, 1, :], ACT.Copy).then_inc(su["high"], 1)
                act.activation(wqH[:, :], wqk[:, 0, :], ACT.Copy).then_inc(su["high"], 1)
                act.wait_ge(su["dt_neg"], 1)
                act.activation(dtx[:, 1, :], dtx[:, 1, :], ACT.Exp).then_inc(su["dt_exp"], 1)
                act.wait_ge(ld_x, 16)
                act.activation(xfH[:, L:], xf[:, L:], ACT.Copy).then_inc(su["high"], 1)
                act.wait_ge(su["dt_p"], 1)

            def sums():
                act.wait_ge(su["end_d"], 1)
                act.activation(sc[:, :, 2, :], sc[:, :, 2, :], ACT.Exp).then_inc(su["end_exp"], 1)
                act.wait_ge(su["end_p"], 1)
                act.activation(sc[:, :, 3, :], M[2][:, 0:NB * NT * NH].rearrange("p (b c) -> p b c", b=NB),
                               ACT.Exp).then_inc(su["total"], 1)
                act.wait_ge(su["low"], 6)

            def keys():
                for g in range(G):
                    act.wait_ge(su["key_p"], g + 1)
                    if g:
                        act.wait_ge(su["keyS"], g)
                    act.activation(k32, KB[g][:, 0:NB * S], ACT.Identity,
                                   bias=sm[:, BK + g:BK + g + 1]).then_inc(su["key32"], 1)

            def setup_experts():
                act.wait_ge(ld_moe, 48)
                act.activation(w1H[:, 0, :], w1s[:, 0, :], ACT.Copy, scale=0.5).then_inc(su["moeH"], 1)
                act.activation(w1H[:, 1, :], w1s[:, 1, :], ACT.Copy).then_inc(su["moeH"], 1)
                act.activation(w1s[:, 0, :], w1s[:, 0, :], ACT.Copy, scale=0.5).then_inc(su["moeH"], 1)

            def expert_out(m, e):
                reach(act, "w2d", m, FC * e + FC)
                reach(act, "yadd", m, e - 1)
                if e == 0:
                    reach(act, "lgv", m, 10)
                for t in range(NT):
                    i = act.mul(ye[:, e % 2, t * D:(t + 1) * D], Y[:, t * D:(t + 1) * D], lg[:, 5, t, e:e + 1])
                i.then_inc(done["ye_r"], 1)

            def unit(m, u):
                if u >= 4 and u % 2 == 0:
                    expert_out(m, u // 2 - 2)
                reach(act, "ab", m, 2 * u + 1)
                reach(act, "moe_h", m, u - 1)
                act.activation(mt_u[:, u % 2, :], M[2 * u % 3][:, :], ACT.Tanh).then_inc(done["tanh_m"], 1)

            def units(m, which):
                if m is not None:
                    for u in which:
                        unit(m, u)

            def experts_end(m):
                expert_out(m, E - 2)
                expert_out(m, E - 1)

            def columns(m):
                reach(act, "x2T", m, 1)
                act.activation(x2H[:, :], F[0][:, :], ACT.Copy).then_inc(done["x2h"], 1)
                act.copy(x2c[:, :], F[0][:, :]).then_inc(done["x2c_r"], 1)

            def router(m):
                reach(act, "lgv", m, 2)
                act.activation(lg[:, 1, :, :], lg[:, 0, :, :], ACT.Exp).then_inc(done["lexp"], 1)

            def front(b, m):
                def row_sums():
                    for h in range(NH):
                        reach(act, "csb", b, h + 1)
                        reach(act, "csd_r", b - 1, 2)
                        act.activation(ecs[:, h, :], F[1 + h][0:NS, :], ACT.Exp).then_inc(done["ecs_r"], 1)

                def decays():
                    reach(act, "scb_r", b, 1)
                    for h in range(NH):
                        for c in range(NT):
                            act.activation(dd[:, h, c * P:(c + 1) * P], F[1 + h][:, c * P:(c + 1) * P], ACT.Relu,
                                           bias=scb[:, 0, NH * c + h:NH * c + h + 1], scale=-1.0).then_inc(done["dd_r"], 1)
                    for h in range(NH):
                        reach(act, "dd_r", b, NT * (h + 1))
                        act.activation(dd[:, h, :], dd[:, h, :], ACT.Exp, scale=-1.0).then_inc(done["dec"], 1)

                def gate():
                    for h in range(NH):
                        reach(act, "proj", b, 4 + h)
                        reach(act, "gz_r", b - 1, 2)
                        act.activation(gz[:, h, :], F[(3, 0)[h]][:, :], ACT.Tanh).then_inc(done["tanh_z"], 1)

                def silu_x():
                    for k, i in enumerate(LAST_TAP):
                        reach(act, "conv", b, 7 + k)
                        act.activation(xs[:, i, :], acc[:, i, :], ACT.Tanh).then_inc(done["tanh_c"], 1)

                for i in range(NC):
                    reach(act, "proj", b, i + 1)
                    reach(act, "conv", b - 1, 9)
                    act.activation(raw[:, i, TAPS - 1:], F[1 + i][:, :], ACT.Copy).then_inc(done["raw_c"], 1)
                    reach(act, "xs_r", b - 1, 3)
                    act.activation(acc[:, i, :], F[1 + i][:, :], ACT.Identity,
                                   bias=cwh[:, NC * TAPS + i:NC * TAPS + i + 1],
                                   scale=cwh[:, TAPS * i + 3:TAPS * i + 4]).then_inc(done["tap0"], 1)
                if m is None:
                    high_parts()
                    gate()
                    silu_x()
                    sums()
                    row_sums()
                    decays()
                else:
                    row_sums()
                    columns(m)
                    gate()
                    decays()
                    units(m, AT_CONV[0:1])
                    router(m)
                    silu_x()
                units(m, AT_CONV[1:])
                for h in range(NH):
                    reach(act, "xtT", b, h + 1)
                    for c in range(NT):
                        i = act.mul(xtok(h, c), F[(3, 0)[h]][:, c * P:(c + 1) * P],
                                    scb[:, 1, NH * c + h:NH * c + h + 1])
                    i.then_inc(done["xtok_r"], 1)
                units(m, AT_SCAN)
                if m is None:
                    keys()
                    setup_experts()
                units(m, AT_GATE)
                units(m, AT_NORM)
                reach(act, "x1T", b, 1)
                act.activation(x1H[:, :], F[3][:, :], ACT.Copy).then_inc(done["x1h"], 1)
                for g in range(G):
                    reach(act, "qdot", b, g + 1)
                    reach(act, "qst_r", b, g - 1)
                    act.activation(q32[:, g % 2, :], F[g][:, :], ACT.Identity,
                                   bias=sm[:, BQ + g:BQ + g + 1]).then_inc(done["q32_r"], 1)
                units(m, AT_QUERY)
                units(m, AT_MAX)
                reach(act, "mT", b, 1)
                act.activation(mt[0:2 * HA, :], F[0][0:2 * HA, :], ACT.Copy).then_inc(done["mt_r"], 1)
                for h in range(HA):
                    g, j = divmod(h, J)
                    reach(act, "ksc", b, h + 1)
                    if g >= 2 and j == 0:
                        reach(act, "pv", b, g - 1)
                    act.activation(pr[0:S, g % 2, j, :], F[h % 2][0:S, :], ACT.Exp, scale=SCALE).then_inc(done["prob"], 1)
                    if j == 1:
                        units(m, at_score(g))
                if m is not None:
                    experts_end(m)
                reach(act, "att_r", b, 1)
                act.activation(att[:, :], att[:, :], ACT.Identity, bias=sm[:, BV:BV + 1]).then_inc(done["attb_r"], 1)

            setup()
            front(0, None)
            with act.Fori(1, NB) as b:
                front(b, b - 1)
            columns(NB - 1)
            router(NB - 1)
            for u in range(U):
                unit(NB - 1, u)
            experts_end(NB - 1)

        @block.vector
        def _(dve):
            def f32(ap):
                return ap.bitcast(F32)

            def over(ap, n):
                return ap.unsqueeze(1).broadcast_to([ap.shape[0], n, ap.shape[1]])

            def log1p():
                u, s, z, r = dtx[:, 1, :], dtx[:, 2, :], dtx[:, 3, :], dtx[:, 4, :]
                steps = [0]

                def then(i):
                    i.then_inc(su["log1p"], 1)
                    steps[0] += 1
                    dve.wait_ge(su["log1p"], steps[0])

                dve.wait_ge(su["dt_exp"], 1)
                then(dve.tensor_scalar(z, u, 2.0, None, ALU.add))
                then(dve.reciprocal(z, z))
                then(dve.tensor_tensor(s, u, z, ALU.mult))
                then(dve.tensor_tensor(z, s, s, ALU.mult))
                then(dve.tensor_scalar(r, z, 1.0 / (2 * LOG_TERMS + 1), None, ALU.mult))
                for k in range(LOG_TERMS - 1, 0, -1):
                    then(dve.scalar_tensor_tensor(r, r, 1.0 / (2 * k + 1), z, ALU.add, ALU.mult))
                then(dve.tensor_scalar(r, r, 1.0, 2.0, ALU.add, ALU.mult))
                then(dve.tensor_tensor(u, r, s, ALU.mult))

            def setup():
                dve.wait_ge(ld_c, 32)
                dve.tensor_scalar(cwh[:, :], sm[:, CW:CW + NC * TAPS + NC], 0.5, None, ALU.mult).then_inc(su["taps"], 1)
                dve.wait_ge(su["high"], 2)
                dve.scalar_tensor_tensor(winL[:, WZ:WX], win[:, WZ:WX], 0.5, f32(winH[:, WZ:WX]),
                                         ALU.mult, ALU.subtract).then_inc(su["low"], 1)
                dve.tensor_tensor(winL[:, WX:WDT], win[:, WX:WDT], f32(winH[:, WX:WDT]), ALU.subtract).then_inc(su["low"], 1)
                dve.wait_ge(su["high"], 3)
                dve.tensor_tensor(xfL[:, 0:L], xf[:, 0:L], f32(xfH[:, 0:L]), ALU.subtract).then_inc(su["low"], 1)
                dve.wait_ge(su["zero"], 1)

            def steps():
                dve.wait_ge(su["dt_p"], 1)
                dve.tensor_tensor(dtx[:, 0, :].rearrange("p (t h) -> p t h", h=NH),
                                  M[0][:, 0:NB * NT * NH].rearrange("p (t h) -> p t h", h=NH),
                                  over(sm[:, DTB:DTB + NH], NB * NT), ALU.add).then_inc(su["dt_x"], 1)
                dve.wait_ge(su["dt_x"], 1)
                dve.scalar_tensor_tensor(dtx[:, 1, :], dtx[:, 0, :], -1.0, dtx[:, 0, :], ALU.mult, ALU.min).then_inc(su["dt_neg"], 1)
                dve.wait_ge(su["high"], 6)
                dve.tensor_tensor(cxL, cx, f32(cxH), ALU.subtract).then_inc(su["low"], 1)
                dve.tensor_tensor(wkL, wqk[:, 1, :], f32(wkH), ALU.subtract).then_inc(su["low"], 1)
                dve.tensor_tensor(wqL[:, :], wqk[:, 0, :], f32(wqH[:, :]), ALU.subtract).then_inc(su["low"], 1)
                log1p()
                dve.scalar_tensor_tensor(sc[:, :, 1, :], dtx[:, 0, :].rearrange("p (b c) -> p b c", b=NB), 0.0,
                                         dtx[:, 1, :].rearrange("p (b c) -> p b c", b=NB),
                                         ALU.max, ALU.add).then_inc(su["dt"], 1)
                dve.wait_ge(su["dt"], 1)
                dve.wait_ge(su["aexp"], 1)
                for b in range(NB):
                    i = dve.scalar_tensor_tensor(
                        dta[:, b * NT * NH:(b + 1) * NT * NH].rearrange("p (t h) -> p t h", h=NH),
                        sc[:, b, 1, :].rearrange("p (t h) -> p t h", h=NH), -1.0, over(aexp[:, :], NT),
                        ALU.mult, ALU.mult)
                i.then_inc(su["dta"], 1)
                dve.wait_ge(su["dta"], 1)
                dve.tensor_scalar(dta[:, :], dta[:, :], UNDERFLOW, None, ALU.max).then_inc(su["dta"], 1)
                dve.wait_ge(su["high"], 7)
                dve.tensor_tensor(xfL[:, L:], xf[:, L:], f32(xfH[:, L:]), ALU.subtract).then_inc(su["low"], 1)

            def sums():
                dve.wait_ge(su["cs_p"], 1)
                dve.tensor_copy(sc[:, :, 0, :], M[1][:, 0:NB * NT * NH].rearrange("p (b c) -> p b c", b=NB)).then_inc(su["cs"], 1)
                dve.wait_ge(su["cs"], 1)
                dve.wait_ge(su["end_p"], 1)
                dve.tensor_tensor(sc[:, :, 2, :], M[2][:, 0:NB * NT * NH].rearrange("p (b c) -> p b c", b=NB),
                                  sc[:, :, 0, :], ALU.subtract).then_inc(su["end_d"], 1)

            def keys():
                for g in range(G):
                    dve.wait_ge(su["key32"], g + 1)
                    if g:
                        dve.wait_ge(su["key_in"], g)
                    dve.tensor_copy(kH, k32).then_inc(su["keyH"], 1)
                    dve.wait_ge(su["keyH"], g + 1)
                    dve.scalar_tensor_tensor(kst0, f32(kH), con[:, MK:MK + 1], k32,
                                             ALU.mult, ALU.add).then_inc(su["keyS"], 1)
                    dve.wait_ge(su["keyS"], g + 1)
                    dve.tensor_scalar(kc[:, :, g, :], kst0.rearrange("p (b s) -> p b s", b=NB),
                                      con[:, KEEP:KEEP + 1], None, ALU.mult).then_inc(su["key_in"], 1)

            def values_in():
                dve.wait_ge(su["val_p"], 1)
                dve.tensor_copy(vc[:, :, :], M[0][0:S, :].rearrange("p (b d) -> p b d", b=NB)).then_inc(su["val_in"], 1)

            def unit(m, u):
                a, k = M[2 * u % 3], M[(2 * u + 1) % 3]
                reach(dve, "tanh_m", m, u + 1)
                dve.scalar_tensor_tensor(mt_u[:, u % 2, :], mt_u[:, u % 2, :], 1.0, a[:, :],
                                         ALU.add, ALU.mult).then_inc(done["moe_u"], 1)
                reach(dve, "moe_u", m, u + 1)
                reach(dve, "ab", m, 2 * u + 2)
                reach(dve, "w2d", m, u - 2)
                dve.tensor_tensor(mt_h[:, u % 3, :], mt_u[:, u % 2, :], k[:, :], ALU.mult).then_inc(done["moe_h"], 1)

            def units(m, which):
                if m is not None:
                    for u in which:
                        unit(m, u)

            def statistics(k, b):
                if k == 2:
                    reach(dve, "yadd", b, E)
                else:
                    reach(dve, f"res{k}", b, 1)
                for t in range(NT):
                    dve.bn_stats(bst[:, k, t, :], res[k][:, t, :]).then_inc(done[f"stat{k}"], 1)
                for t in range(NT):
                    reach(dve, f"stat{k}", b, t + 1, alone=True)
                    dve.bn_aggr(mv[:, k, t, :], bst[:, k, t, :]).then_inc(done[f"mv{k}"], 1)

            def normalise(k, b, out):
                reach(dve, f"mv{k}", b, NT)
                reach(dve, f"rstd{k}", b, 1)
                for t in range(NT):
                    dve.tensor_scalar(out[:, t, :], res[k][:, t, :], mv[:, k, t, 0:1], rstd[:, k, 1, t:t + 1],
                                      ALU.subtract, ALU.mult).then_inc(done[f"norm{k}"], 1)

            def front(b, m):
                if m is not None:
                    add_attention(m)
                for s, k in enumerate((2, 1, 0)):
                    if s == 1 and m is not None:
                        normalise(1, m, res[1])
                    if s == 2 and m is not None:
                        low_columns(m)
                        router_logits(m)
                    for i in range(NC) if s < 2 else LAST_TAP:
                        if s == 0:
                            reach(dve, "tap0", b, i + 1)
                        else:
                            reach(dve, "conv", b, NC * (s - 1) + i + 1)
                        dve.scalar_tensor_tensor(acc[:, i, :], raw[:, i, k:k + L], cwh[:, TAPS * i + k:TAPS * i + k + 1],
                                                 acc[:, i, :], ALU.mult, ALU.add).then_inc(done["conv"], 1)
                if m is None:
                    steps()
                for h in range(NH):
                    reach(dve, "tanh_z", b, h + 1)
                    dve.scalar_tensor_tensor(gz[:, h, :], gz[:, h, :], 1.0, F[(3, 0)[h]][:, :],
                                             ALU.add, ALU.mult).then_inc(done["gz_r"], 1)
                units(m, AT_CONV[0:1])
                if m is None:
                    sums()
                if not isinstance(b, int):
                    dve.wait_ge(c_low, 16 * b)
                for k, i in enumerate(LAST_TAP):
                    reach(dve, "tanh_c", b, k + 1)
                    dve.scalar_tensor_tensor(xs[:, i, :], xs[:, i, :], 1.0, acc[:, i, :],
                                             ALU.add, ALU.mult).then_inc(done["xs_r"], 1)
                units(m, AT_CONV[1:2])
                if m is not None:
                    router(m)
                units(m, AT_CONV[2:])
                reach(dve, "btT", b, 1)
                for h in range(NH):
                    for c in range(NT - 1):
                        dve.tensor_scalar(bw[:, h, c, :], F[1][:, c * NS:(c + 1) * NS],
                                          scb[:, 2, NH * c + h:NH * c + h + 1], None, ALU.mult).then_inc(done["bw_r"], 1)
                reach(dve, "gdot", b, 1)
                dve.tensor_tensor(gm[:, :].rearrange("p (c q) -> p c q", c=NT),
                                  F[2][:, :].rearrange("p (c q) -> p c q", c=NT), over(tri, NT),
                                  ALU.mult).then_inc(done["gm_r"], 1)
                units(m, AT_SCAN)
                reach(dve, "gm_r", b, 1)
                for h in range(NH):
                    reach(dve, "dec", b, h + 1)
                    dve.tensor_tensor(dd[:, h, :], dd[:, h, :], gm[:, :], ALU.mult).then_inc(done["m_r"], 1)
                for c in range(NT - 1):
                    for h in range(NH):
                        new = F[(1, 3)[h]][0:NS, c * P:(c + 1) * P]
                        if c == 0:
                            reach(dve, "upd", b, h + 1)
                            i = dve.tensor_copy(st[:, h, 0, :], new)
                        else:
                            reach(dve, "s_r", b, NH * (c - 1) + h + 1)
                            i = dve.scalar_tensor_tensor(st[:, h, c, :], st[:, h, c - 1, :],
                                                         scb[0:NS, 3, NH * c + h:NH * c + h + 1], new,
                                                         ALU.mult, ALU.add)
                        i.then_inc(done["s_r"], 1)
                for h in range(NH):
                    reach(dve, "ydot", b, h + 1)
                    dve.scalar_tensor_tensor(y1[:, h, :], xs[:, h, :], sm[:, DSK + h:DSK + h + 1],
                                             F[(0, 2)[h]][:, :], ALU.mult, ALU.add).then_inc(done["y1_r"], 1)
                units(m, AT_GATE)
                if m is None:
                    keys()
                reach(dve, "wout_d", b, 1)
                dve.wait_ge(ld_tok, 16 * (b + 1))
                dve.tensor_tensor(res[0][:, :, :], F[1][:, :].rearrange("p (t d) -> p t d", t=NT),
                                  xt[:, :, :], ALU.add).then_inc(done["res0"], 1)
                statistics(0, b)
                units(m, AT_NORM[0:1])
                if m is None:
                    values_in()
                normalise(0, b, x1)
                units(m, AT_NORM[1:])
                reach(dve, "x1h", b, 1)
                dve.tensor_tensor(x1L[:, :], F[3][:, :], f32(x1H[:, :]), ALU.subtract).then_inc(done["x1l"], 1)
                for g in range(G):
                    reach(dve, "q32_r", b, g + 1)
                    dve.tensor_copy(qst[:, g, :], q32[:, g % 2, :]).then_inc(done["qh_r"], 1)
                    reach(dve, "qh_r", b, g + 1)
                    dve.scalar_tensor_tensor(qst[:, g, :], f32(qst[:, g, :]), con[:, MQ:MQ + 1], q32[:, g % 2, :],
                                             ALU.mult, ALU.add).then_inc(done["qst_r"], 1)
                units(m, AT_QUERY)
                for i in range(NT * G):
                    t, g = divmod(i, G)
                    if i == 12:
                        units(m, AT_MAX[0:1])
                    reach(dve, "tsc", b, i + 1)
                    dve.tensor_reduce(smax[:, t, J * g:J * g + J], F[g][:, 0:J * S].rearrange("p (j s) -> p j s", j=J),
                                      AX.X, ALU.max).then_inc(done["tmax"], 1)
                reach(dve, "tmax", b, NT * G)
                dve.tensor_copy(smH[:, :, :], smax[:, :, :]).then_inc(done["msplit"], 1)
                reach(dve, "msplit", b, 1)
                dve.tensor_copy(smHL[:, :, 0, :], f32(smH[:, :, :])).then_inc(done["msplit"], 1)
                dve.tensor_tensor(smHL[:, :, 1, :], smax[:, :, :], f32(smH[:, :, :]), ALU.subtract).then_inc(done["msplit"], 1)
                units(m, AT_MAX[1:])
                units(m, AT_SCORE)
                if m is None:
                    dve.wait_ge(su["moeH"], 3)
                    dve.tensor_tensor(w1L[:, 0, :], w1s[:, 0, :], f32(w1H[:, 0, :]), ALU.subtract).then_inc(su["moeL"], 1)
                reach(dve, "pv", b, G)
                dve.reciprocal(rsum[:, :], F[3][:, :]).then_inc(done["rs_r"], 1)
                reach(dve, "rs_r", b, 1)
                dve.tensor_tensor(att[:, :], F[2][:, :], rsum[:, :], ALU.mult).then_inc(done["att_r"], 1)
                if m is not None:
                    statistics(2, m)

            def add_attention(b):
                reach(dve, "wo_d", b, 1)
                reach(dve, "bo_r", b, 1)
                dve.tensor_tensor(res[1][:, :, :], F[0][:, :].rearrange("p (t d) -> p t d", t=NT),
                                  x1bo[:, :, :], ALU.add).then_inc(done["res1"], 1)
                statistics(1, b)

            def low_columns(b):
                reach(dve, "x2h", b, 1)
                reach(dve, "x2c_r", b, 1)
                dve.tensor_tensor(x2L[:, :], F[0][:, :], f32(x2H[:, :]), ALU.subtract).then_inc(done["x2l"], 1)

            def per_expert(ap):
                return ap.unsqueeze(2).broadcast_to([P, NT, E])

            def router_logits(b):
                logits = Y[:, 0:NT * E].rearrange("p (t e) -> p t e", t=NT)
                reach(dve, "logit", b, 1)
                dve.tensor_reduce(lmx[:, 0, :], logits, AX.X, ALU.max).then_inc(done["lgv"], 1)
                reach(dve, "lgv", b, 1)
                dve.tensor_tensor(lg[:, 0, :, :], logits, per_expert(lmx[:, 0, :]), ALU.subtract).then_inc(done["lgv"], 1)

            def router(b):
                step = [2]

                def then(i, alone=False):
                    i.then_inc(done["lgv"], 1)
                    step[0] += 1
                    reach(dve, "lgv", b, step[0], alone)

                reach(dve, "lexp", b, 1)
                then(dve.tensor_reduce(lmx[:, 1, :], lg[:, 1, :, :], AX.X, ALU.add))
                then(dve.reciprocal(lmx[:, 2, :], lmx[:, 1, :]))
                then(dve.tensor_tensor(lg[:, 2, :, :], lg[:, 1, :, :], per_expert(lmx[:, 2, :]), ALU.mult), alone=True)
                for t in range(NT):
                    dve.max(top[:, t, :], lg[:, 2, t, :]).then_inc(done["topv"], 1)
                for t in range(NT):
                    reach(dve, "topv", b, t + 1, alone=True)
                    dve.max_index(topi[:, t, :], top[:, t, :], lg[:, 2, t, :]).then_inc(done["topv"], 1)
                reach(dve, "topv", b, 2 * NT)
                then(dve.tensor_copy(topf[:, :, :], topi[:, :, :]))
                then(dve.tensor_tensor(lmx[:, 1, :], top[:, :, 0], top[:, :, 1], ALU.add))
                then(dve.reciprocal(lmx[:, 3, :], lmx[:, 1, :]))
                iota = con[:, IOTA:IOTA + E]
                for t in range(NT):
                    dve.tensor_scalar(lg[:, 3, t, :], iota, topf[:, t, 0:1], None, ALU.is_equal).then_inc(done["topv"], 1)
                for t in range(NT):
                    reach(dve, "topv", b, 2 * NT + t + 1)
                    dve.scalar_tensor_tensor(lg[:, 3, t, :], iota, topf[:, t, 1:2], lg[:, 3, t, :],
                                             ALU.is_equal, ALU.add).then_inc(done["topv"], 1)
                reach(dve, "topv", b, 4 * NT)
                then(dve.tensor_tensor(lg[:, 4, :, :], lg[:, 2, :, :], lg[:, 3, :, :], ALU.mult))
                then(dve.tensor_tensor(lg[:, 5, :, :], lg[:, 4, :, :], per_expert(lmx[:, 3, :]), ALU.mult))

            setup()
            front(0, None)
            with dve.Fori(1, NB) as b:
                front(b, b - 1)
            add_attention(NB - 1)
            normalise(1, NB - 1, res[1])
            low_columns(NB - 1)
            router_logits(NB - 1)
            router(NB - 1)
            for u in range(U):
                unit(NB - 1, u)
            statistics(2, NB - 1)

        @block.gpsimd
        def _(pool):
            def setup():
                pool.memset(half[:, :], -0.5).then_inc(su["half"], 1)
                pool.memset(raw[:, :, 0:TAPS - 1], 0.0).then_inc(su["zero"], 1)
                pool.memset(kst[:, :, :].bitcast(F32), 0.0).then_inc(su["zero"], 1)
                pool.memset(vst[:, :, :], 0.0).then_inc(su["zero"], 1)
                pool.memset(mt[:, :].bitcast(F32), 0.0).then_inc(su["zero"], 1)
                pool.wait_ge(su["zero"], 4)
                pool.memset(pr[64:P, :, :, :], 0.0).then_inc(su["zero"], 1)
                pool.wait_ge(su["zero"], 5)
                pool.wait_ge(ld_c, 32)
                pool.tensor_copy(sel[:, :], con[:, IND:IND + HA + E]).then_inc(su["sel"], 1)

            def setup_experts():
                pool.wait_ge(su["moeH"], 2)
                pool.tensor_tensor(w1L[:, 1, :], w1s[:, 1, :], w1H[:, 1, :].bitcast(F32), ALU.subtract).then_inc(su["moeLv"], 1)

            def static_copies(b):
                if isinstance(b, int):
                    pool.wait_ge(su["key_in"], G)
                    pool.wait_ge(su["val_in"], 1)
                    pool.wait_ge(su["zero"], 3)
                    pool.wait_ge(done["rstd0"], 1)
                else:
                    reach(pool, "scb_r", b, 1)
                for j in range(J):
                    reach(pool, "copies", b, j)
                    rows = slice(32 * j, 32 * j + 32)
                    pool.tensor_copy(kst[rows, j:HA:J, :], kc[rows, b, :, :]).then_inc(done["copies"], 1)
                reach(pool, "copies", b, J)
                for g in range(G):
                    pool.tensor_copy(vst[0:S, J * g:J * g + J, DH * g:DH * g + DH],
                                     vc[:, b, 32 * g:32 * g + 32].rearrange("p (j d) -> p j d", j=J)).then_inc(done["copies"], 1)

            def expert_add(m, e):
                reach(pool, "yadd", m, e)
                reach(pool, "ye_r", m, e + 1)
                if e == 0 and isinstance(m, int):
                    pool.wait_ge(stored, 16 * m)
                elif e == 0:
                    pool.wait_ge(ld_tok, 16 * (m + 2))
                pool.tensor_tensor(res[2][:, :, :], ye[:, e % 2, :].rearrange("p (t d) -> p t d", t=NT),
                                   res[1 if e == 0 else 2][:, :, :], ALU.add).then_inc(done["yadd"], 1)

            def unit(m, u):
                if u >= 4 and u % 2 == 0:
                    expert_add(m, u // 2 - 2)

            def experts_end(m):
                expert_add(m, E - 2)
                expert_add(m, E - 1)
                deviation(2, m)
                reach(pool, "rstd2", m, 1, alone=True)
                for t in range(NT):
                    pool.tensor_scalar(res[2][:, t, :], res[2][:, t, :], mv[:, 2, t, 0:1], rstd[:, 2, 1, t:t + 1],
                                       ALU.subtract, ALU.mult).then_inc(done["norm2"], 1)

            def units(m, which):
                if m is not None:
                    for u in which:
                        unit(m, u)

            def deviation(k, b):
                reach(pool, f"mv{k}", b, NT, alone=True)
                pool.tensor_scalar(rstd[:, k, 0, :], mv[:, k, :, 1], EPS, None, ALU.add).then_inc(done[f"eps{k}"], 1)
                reach(pool, f"eps{k}", b, 1)
                pool.tensor_tensor(rstd[:, k, 1, :], rstd[:, k, 0, :], half[:, :], ALU.pow).then_inc(done[f"rstd{k}"], 1)
            def front(b, m):
                reach(pool, "wo_d", b - 1, 1)
                pool.tensor_copy(scb[:, :, :], sc[:, b, :, :]).then_inc(done["scb_r"], 1)
                if m is not None:
                    deviation(1, m)
                if m is not None:
                    static_copies(b)
                units(m, AT_CONV)
                pool.wait_ge(c_low, 16 * (b + 1))
                for h in range(NH):
                    reach(pool, "ecs_r", b, h + 1)
                    pool.tensor_tensor(ecs[:, h, :], clow[:, :], ecs[:, h, :], ALU.mult).then_inc(done["csd_r"], 1)
                units(m, AT_SCAN)
                for h in range(NH):
                    reach(pool, "y1_r", b, h + 1)
                    pool.tensor_tensor(y1[:, h, :], y1[:, h, :], gz[:, h, :], ALU.mult).then_inc(done["yg_r"], 1)
                units(m, AT_GATE)
                deviation(0, b)
                if m is None:
                    static_copies(b)
                units(m, AT_NORM)
                reach(pool, "norm0", b, NT)
                pool.tensor_tensor(x1bo[:, :, :], x1[:, :, :], bo[:, :].unsqueeze(1).broadcast_to([P, NT, D]),
                                   ALU.add).then_inc(done["bo_r"], 1)
                if m is None:
                    setup_experts()
                units(m, AT_QUERY)
                units(m, AT_MAX)
                units(m, AT_SCORE)
                if m is not None:
                    experts_end(m)

            setup()
            pool.wait_ge(su["end_exp"], 1)
            pool.wait_ge(su["total"], 1)
            pool.wait_ge(ld_late, 64)
            front(0, None)
            with pool.Fori(1, NB) as b:
                front(b, b - 1)
            deviation(1, NB - 1)
            for u in range(U):
                unit(NB - 1, u)
            experts_end(NB - 1)


def kernel(**inputs):
    import concourse.bacc as bacc
    from concourse.bass_utils import run_bass_kernel_spmd

    a = {k: np.asarray(v) for k, v in inputs.items()}
    heads = np.arange(HA).reshape(G, J)
    stacked = (heads[:, :, None] * DH + (np.arange(32) % DH)[None, None, :]).reshape(-1)
    packed = (heads.T[:, :, None] * DH + np.arange(DH)[None, None, :]).reshape(-1)
    x = a["x"].reshape(NB * L, D)
    small = np.concatenate([
        a["L0_attn_conv_w"].reshape(NC, P, TAPS).transpose(1, 0, 2).reshape(P, NC * TAPS),
        a["L0_attn_conv_b"].reshape(NC, P).T,
        np.broadcast_to(a["L0_attn_A_log"], (P, NH)),
        np.broadcast_to(a["L0_attn_dt_bias"], (P, NH)),
        np.broadcast_to(a["L0_attn_D_skip"], (P, NH)),
        a["L0_xattn_bq"][stacked].reshape(G, P).T,
        a["L0_xattn_bk"][stacked].reshape(G, P).T,
        a["L0_xattn_bv"][packed].reshape(P, 1),
    ], axis=1)
    arrays = {
        "x_feat": x.T,
        "x_tok": x.reshape(NB, NT, P, D).transpose(2, 0, 1, 3),
        "ctx_feat": a["ctx_1024"].reshape(NB * S, D).T,
        "small": small,
        "cst": constants(),
        "bo_row": np.broadcast_to(a["L0_xattn_bo"], (P, D)),
        "w_in": a["L0_attn_W_in"].T,
        "w_out": a["L0_attn_W_out"].T.reshape(NH, P, D).transpose(1, 0, 2),
        "wq": a["L0_xattn_Wq"].T[:, stacked],
        "wk": a["L0_xattn_Wk"].T[:, stacked],
        "wv": a["L0_xattn_Wv"].T,
        "wo": a["L0_xattn_Wo"].T[packed, :],
        "router": a["L0_ffn_router_w"].T,
        "w1": a["L0_ffn_w1"].transpose(2, 0, 1).reshape(D, E * FC * P),
        "v1": a["L0_ffn_v1"].transpose(2, 0, 1).reshape(D, E * FC * P),
        "w2": a["L0_ffn_w2"].reshape(E * FC, P, D).transpose(1, 0, 2),
    }
    arrays = {k: np.ascontiguousarray(v) for k, v in arrays.items()}
    nc = bacc.Bacc("TRN2", target_bir_lowering=False, num_devices=1)
    args = {k: nc.dram_tensor(k, v.shape, mybir.dt.from_np(v.dtype), kind="ExternalInput").ap()
            for k, v in arrays.items()}
    out = nc.dram_tensor("out", (P, NB, NT, D), F32, kind="ExternalOutput").ap()
    decoder_kernel(nc, **args, out=out)
    r = run_bass_kernel_spmd(nc, [arrays], core_ids=[0])
    return r.results[0]["out"].transpose(1, 2, 0, 3).reshape(NB, L, D)
```

```python
from contextlib import ExitStack

import numpy as np
import concourse.bass as bass
from concourse import mybir

F32 = mybir.dt.float32
F32R = mybir.dt.float32r
U32 = mybir.dt.uint32
ALU = mybir.AluOpType
ACT = mybir.ActivationFunctionType
AX = mybir.AxisListType

P = 128
NB, L, D = 4, 512, 128
NT = L // P
NS = 64
NC = 3
TAPS = 4
NH = 2
HA, DH, G, J = 16, 8, 4, 4
S = 77
E, FC = 8, 2
U = E * FC
EPS = 1e-5
UNDERFLOW = -110.0
LOG_TERMS = 8
SCALE = float(DH) ** -0.5
CW, CB, ALOG, DTB, DSK, BQ, BK = 0, 12, 15, 17, 19, 21, 25
NSMALL = 29
IDENT, TRI, LAST, ONES, MQ, MK, KEEP, IND, SELC, IOTA = 0, 128, 256, 384, 512, 513, 514, 515, 531, 539
NCST = 547
WZ, WX, WDT = 0, 256, 640


def constants():
    c = np.zeros((P, NCST), np.float32)
    p = np.arange(P)
    c[:, IDENT:IDENT + P] = np.eye(P)
    c[:, TRI:TRI + P] = p[:, None] <= p[None, :]
    c[P - 1, LAST:LAST + P] = 1.0
    for g in range(G):
        c[:S, ONES + 32 * g + 8 * g:ONES + 32 * g + 8 * g + 8] = 1.0
    r = p % 32
    c[:, MQ] = -1.0 * ((r >= 8) & (r < 16))
    c[:, MK] = -1.0 * ((r >= 16) & (r < 24))
    c[:, KEEP] = r < 24
    for h in range(HA):
        c[h, IND + h] = c[HA + h, IND + h] = -1.0
    for e in range(E):
        c[e, SELC + e] = c[E + e, SELC + e] = 1.0
    c[:, IOTA:IOTA + E] = np.arange(E)
    return c


def decoder_kernel(nc, x_feat, x_tok, ctx_feat, small, cst, bo_row, w_in, w_out, wq, wk, wv, wo,
                   router, w1, v1, w2, bv_row, out):
    with ExitStack() as ctx:
        def sb(name, shape, dt=F32):
            return ctx.enter_context(nc.sbuf_tensor(name, shape, dt))

        def sem(name):
            return ctx.enter_context(nc.semaphore(name))

        xf = sb("xf", [P, NB * L])
        xfH = sb("xfH", [P, NB * L], F32R)
        xfL = sb("xfL", [P, NB * L], F32R)
        sm = sb("sm", [P, NSMALL])
        con = sb("con", [P, NCST])
        bo = sb("bo", [P, D])
        bv = sb("bv", [S, D])
        winH = sb("winH", [P, 640], F32R)
        winL = sb("winL", [P, 640], F32R)
        wout = sb("wout", [P, NH, D])
        wqH = sb("wqH", [P, G * P], F32R)
        wqL = sb("wqL", [P, G * P], F32R)
        wvs = sb("wvs", [P, D])
        wos = sb("wos", [P, D])
        wr = sb("wr", [P, E])
        w1H = sb("w1H", [P, 2, E * FC * P], F32R)
        w1L = sb("w1L", [P, 2, E * FC * P], F32R)
        w2s = sb("w2s", [P, E * FC, D])
        ident = con[:, IDENT:IDENT + P]
        tri = con[:, TRI:TRI + P]
        last = con[:, LAST:LAST + P]
        ones = con[:, ONES:ONES + P]
        cwh = sb("cwh", [P, NC * TAPS + NC])
        sel = sb("sel", [P, HA + E], F32R)
        aexp = sb("aexp", [P, NH])
        dtx = sb("dtx", [P, 5, NB * NT * NH])
        dta = sb("dta", [P, NB * NT * NH])
        sc = sb("sc", [P, NB, 4, NT * NH])
        kc = sb("kc", [P, NB, G, S], F32R)
        vc = sb("vc", [S, NB, D])
        half = sb("half", [P, NT])
        kst = sb("kst", [P, HA, S], F32R)
        vst = sb("vst", [P, HA, 32])
        scb = sb("scb", [P, 4, NT * NH])
        xt = sb("xt", [P, NT, D])
        raw = sb("raw", [P, NC, TAPS - 1 + L])
        acc = sb("acc", [P, NC, L])
        k32 = sb("k32", [P, G, NB * S])
        xs = sb("xs", [P, NC, L])
        gz = sb("gz", [P, NH, L])
        dd = sb("dd", [P, NH, L])
        bw = sb("bw", [P, NH, NT - 1, NS])
        st = sb("st", [NS, NH, NT - 1, D])
        res = [sb(f"res{k}", [P, NT, D]) for k in range(3)]
        bst = sb("bst", [P, 3, NT, 6])
        mv = sb("mv", [P, 3, NT, 2])
        rstd = sb("rstd", [P, 3, 2, NT])
        x1 = sb("x1", [P, NT, D])
        x1H = sb("x1H", [P, L], F32R)
        x1L = sb("x1L", [P, L], F32R)
        qst = sb("qst", [P, G, L], F32R)
        smax = sb("smax", [P, NT, HA])
        smH = sb("smH", [P, NT, HA], F32R)
        smHL = sb("smHL", [P, NT, 2, HA])
        mt = sb("mt", [P, L], F32R)
        pr = sb("pr", [P, 2, J, L])
        rsum = sb("rsum", [P, L])
        att = sb("att", [P, L])
        x2H = sb("x2H", [P, L], F32R)
        x2L = sb("x2L", [P, L], F32R)
        lg = sb("lg", [P, 6, NT, E])
        lmx = sb("lmx", [P, 4, NT])
        top = sb("top", [P, NT, 8])
        topi = sb("topi", [P, NT, 8], U32)
        topf = sb("topf", [P, NT, 8])
        stage = sb("stage", [P, 8, L])
        mt_u, mt_h, ye = stage[:, 0:2, :], stage[:, 2:5, :], stage[:, 5:7, :]
        win = gz[:, :, :].rearrange("p h l -> p (h l)")[:, 0:642]
        wqk = dd
        wkH, wkL, cxH, cxL = qst[:, 0, :], qst[:, 1, :], qst[:, 2, 0:NB * S], qst[:, 3, 0:NB * S]
        cx = att[:, 0:NB * S]
        kst0 = res[1][:, :, :].rearrange("p t d -> p (t d)")[:, 0:NB * S]
        kH = x2H[:, 0:NB * S]
        w1s = stage[:, :, :].rearrange("p e l -> p (e l)").rearrange("p (w k) -> p w k", w=2)
        y1 = acc
        ecs = pr[0:NS, 0, 0:NH, :]
        clow = pr[0:NS, 0, NH, :]
        x2c = rsum
        q32 = dd
        x1bo = res[0]

        def xtok(h, c):
            return raw[:, h, TAPS - 1 + c * P:TAPS - 1 + (c + 1) * P]

        F = [ctx.enter_context(nc.psum_tensor(f"front{i}", [P, 512], F32)) for i in range(4)]
        M = [ctx.enter_context(nc.psum_tensor(f"moe{i}", [P, 512], F32)) for i in range(3)]
        Y = ctx.enter_context(nc.psum_tensor("moe_y", [P, 512], F32))
        XB = (M[0], M[1], M[2])
        ZB = (M[0], M[1])
        CB = (M[2], F[1])
        TB = (F[3], M[2])
        KB = (M[0], M[1], M[2], Y)

        ld_x0, ld_x, ld_tok, ld_late, ld_ctx, ld_w, ld_c, ld_moe = (sem(n) for n in (
            "ld_x0", "ld_x", "ld_tok", "ld_late", "ld_ctx", "ld_w", "ld_c", "ld_moe"))
        c_low, stored = sem("c_low"), sem("stored")
        su = {n: sem(f"su_{n}") for n in (
            "high", "low", "taps", "dt_p", "dt_x", "dt_neg", "dt_exp", "log1p", "dt", "dta", "aexp",
            "cs_p", "cs", "end_p", "end_d", "end_exp", "total", "key_p", "key32", "keyH",
            "keyS", "key_in", "val_p", "val_in", "zero", "sel", "moeH", "moeL", "moeLv", "half")}

        counts = dict(
            proj=5, csb=2, xtT=2, btT=1, gdot=1, upd=2, ydot=2, wout_d=1, x1T=1, qdot=4, tsc=16,
            mT=1, ksc=HA, pv=4, psum=1, wo_d=1, x2T=1, logit=1, ab=2 * U, w2d=U,
            raw_c=3, tap0=3, tanh_c=3, tanh_z=2, ecs_r=2, dd_r=8, dec=2, xtok_r=2, x1h=1, q32_r=4, mt_r=1,
            prob=HA, x2h=1, x2c_r=1, lexp=1, tanh_m=U, ye_r=E,
            conv=9, xs_r=3, gz_r=2, bw_r=6, m_r=2, s_r=6, y1_r=2,
            res0=1, res1=1, stat0=4, stat1=4, stat2=4, mv0=4, mv1=4, mv2=4,
            norm0=4, norm1=4, norm2=4, x1l=1, qh_r=2, qc_r=2, qst_r=4, tmax=16, msplit=3,
            att_r=2, rs_r=2, x2l=1, lgv=13, topv=8, moe_u=U, moe_h=U,
            scb_r=1, copies=8, mask_r=2, csd_r=2, yg_r=2, bo_r=1, eps0=1, eps1=1, eps2=1, rstd0=1, rstd1=1, rstd2=1,
            yadd=E,
        )
        done = {n: sem(n) for n in counts}

        def reach(eng, name, b, k, alone=False):
            if k <= 0:
                return
            v = counts[name] * b + k
            if not isinstance(v, int):
                if alone:
                    v = eng.to_reg(v)
                    eng.wait_ge(ld_c, 32)
                eng.wait_ge(done[name], v)
            elif v > 0:
                eng.wait_ge(done[name], v)

        def row(b):
            return bass.ds(b * L, L)

        block = ctx.enter_context(nc.Block())
        LAST_TAP = (2, 0, 1)

        AT_COLUMNS, AT_GATE, AT_NORM, AT_QUERY, AT_MAX, AT_SPLIT, AT_ROWS, AT_SCORE = (
            range(0, 2), range(2, 4), range(4, 6), range(6, 8), range(8, 10), range(10, 11), range(11, 12),
            range(12, 16))

        def at_score(h):
            return AT_SCORE[h // 2:h // 2 + 1] if h % 2 else ()

        @block.sync
        def _(sp):
            sp.dma_start(win, w_in).then_inc(ld_w, 16)
            sp.dma_start(xf[:, 0:L], x_feat[:, 0:L]).then_inc(ld_x0, 16)
            sp.dma_start(con[:, :], cst).then_inc(ld_c, 16)
            sp.dma_start(sm[:, :], small).then_inc(ld_c, 16)
            sp.dma_start(xf[:, L:], x_feat[:, L:]).then_inc(ld_x, 16)
            sp.dma_start(cx, ctx_feat).then_inc(ld_ctx, 16)
            sp.dma_start(wqk[:, 1, :], wk).then_inc(ld_ctx, 16)
            sp.dma_start(wqk[:, 0, :], wq).then_inc(ld_ctx, 16)
            sp.dma_start(wvs[:, :], wv).then_inc(ld_ctx, 16)
            sp.dma_start(wout[:, :, :], w_out).then_inc(ld_late, 16)
            sp.dma_start(bo[:, :], bo_row).then_inc(ld_late, 16)
            sp.dma_start(bv[:, :], bv_row).then_inc(ld_late, 16)
            sp.dma_start(wos[:, :], wo).then_inc(ld_late, 16)
            sp.dma_start(wr[:, :], router).then_inc(ld_late, 16)
            sp.dma_start(w1s[:, 0, :], w1).then_inc(ld_moe, 16)
            sp.dma_start(w1s[:, 1, :], v1).then_inc(ld_moe, 16)
            sp.dma_start(w2s[:, :, :], w2).then_inc(ld_moe, 16)

            def load_tokens(b):
                reach(sp, "res0", b - 1, 1)
                sp.dma_start(xt[:, :, :], x_tok[:, b, :, :]).then_inc(ld_tok, 16)

            def lower_c(b):
                reach(sp, "csd_r", b - 1, 2)
                reach(sp, "gdot", b - 1, 1)
                reach(sp, "xs_r", b, 1)
                reach(sp, "pv", b - 1, 3)
                sp.dma_start(clow[:, :], xs[NS:P, 2, :]).then_inc(c_low, 16)

            def store(b):
                reach(sp, "norm2", b, 4)
                sp.dma_start(out[:, b, :, :], res[2][:, :, :]).then_inc(stored, 16)

            load_tokens(0)
            lower_c(0)
            with sp.Fori(1, NB) as b:
                load_tokens(b)
                lower_c(b)
                store(b - 1)
                total = sp.to_reg(16 * b)
                sp.wait_ge(ld_c, 32)
                sp.wait_ge(stored, total)
            store(NB - 1)
            sp.wait_ge(stored, 16 * NB)

        @block.tensor
        def _(pe):
            def split3(o, wH, wL, xH, xL, signal):
                pe.matmul(o, wH, xH, start=True, stop=False)
                pe.matmul(o, wH, xL, start=False, stop=False)
                pe.matmul(o, wL, xH, start=False, stop=True).then_inc(signal, 1)

            def steps():
                pe.wait_ge(ld_x, 16)
                for t in range(NB * NT):
                    mm = pe.matmul(F[0][:, NH * t:NH * t + NH], xf[:, t * P:(t + 1) * P],
                                   win[:, WDT:WDT + NH], start=True, stop=True)
                mm.then_inc(su["dt_p"], 1)

            def sums():
                pe.wait_ge(ld_c, 32)
                pe.wait_ge(su["dta"], 2)
                pe.matmul(F[1][:, 0:NB * NT * NH], tri, dta[:, :], start=True, stop=True).then_inc(su["cs_p"], 1)
                pe.wait_ge(su["cs"], 1)
                pe.matmul(F[2][:, 0:NB * NT * NH].rearrange("p (b c) -> p b c", b=NB), last,
                          sc[:, :, 0, :], start=True, stop=True).then_inc(su["end_p"], 1)

            def keys():
                pe.wait_ge(su["high"], 6)
                pe.wait_ge(su["low"], 6)
                pe.wait_ge(su["end_d"], 1)
                pe.wait_ge(su["total"], 1)
                pe.wait_ge(done["gz_r"], NH)
                pe.wait_ge(done["xtok_r"], NH)
                for g in range(G):
                    split3(KB[g][:, 0:NB * S], wkH[:, g * P:(g + 1) * P], wkL[:, g * P:(g + 1) * P],
                           cxH, cxL, su["key_p"])

            def values_in():
                pe.wait_ge(su["key32"], G)
                for b in range(NB):
                    mm = pe.matmul(M[0][0:S, b * D:(b + 1) * D], cx[:, b * S:(b + 1) * S], wvs[:, :],
                                   start=True, stop=True)
                mm.then_inc(su["val_p"], 1)

            def unit(m, u):
                e, f = divmod(u, FC)
                for which in range(2):
                    k = 2 * u + which
                    if k >= 3:
                        reach(pe, "moe_u" if (k - 3) % 2 == 0 else "moe_h", m, (k - 3) // 2 + 1)
                    w = slice(u * P, (u + 1) * P)
                    if k == 0:
                        reach(pe, "x2h", m, 1)
                    pe.matmul(M[k % 3][:, :], w1H[:, which, w], x2H[:, :], start=True, stop=False)
                    pe.matmul(M[k % 3][:, :], w1L[:, which, w], x2H[:, :], start=False, stop=False)
                    if k == 0:
                        reach(pe, "x2l", m, 1)
                    pe.matmul(M[k % 3][:, :], w1H[:, which, w], x2L[:, :], start=False, stop=True).then_inc(done["ab"], 1)
                if u >= 2:
                    down(m, u - 2)

            def down(m, u):
                if u == 0:
                    reach(pe, "lgv", m, 2)
                elif u % FC == 0:
                    reach(pe, "ye_r", m, u // FC)
                reach(pe, "moe_h", m, u + 1)
                for t in range(NT):
                    mm = pe.matmul(Y[:, t * D:(t + 1) * D], mt_h[:, u % 3, t * P:(t + 1) * P], w2s[:, u, :],
                                   start=(u % FC == 0 and t == 0), stop=(u % FC == FC - 1 and t == NT - 1))
                mm.then_inc(done["w2d"], 1)

            def logits(b):
                reach(pe, "x2c_r", b, 1)
                for t in range(NT):
                    mm = pe.matmul(Y[:, t * E:(t + 1) * E], x2c[:, t * P:(t + 1) * P], wr[:, :],
                                   start=True, stop=True)
                mm.then_inc(done["logit"], 1)

            def experts_end(m):
                down(m, U - 2)
                down(m, U - 1)

            def units(m, which):
                if m is not None:
                    for u in which:
                        unit(m, u)

            def columns(m):
                reach(pe, "norm1", m, 4)
                for t in range(NT):
                    mm = pe.transpose(F[0][:, t * P:(t + 1) * P], res[1][:, t, :], ident)
                mm.then_inc(done["x2T"], 1)

            def attention_out(b):
                for t in range(NT):
                    if t % 2 == 0:
                        reach(pe, "att_r", b, 1 + t // 2)
                    mm = pe.matmul(F[0][:, t * D:(t + 1) * D], att[:, t * P:(t + 1) * P], wos[:, :],
                                   start=True, stop=True)
                mm.then_inc(done["wo_d"], 1)

            def project(bank, b, col):
                split3(bank[:, :], winH[:, col:col + P], winL[:, col:col + P],
                       xfH[:, row(b)], xfL[:, row(b)], done["proj"])

            def project_x(b):
                for i in range(NC):
                    project(XB[i], b, WX + i * P)

            def project_z(b):
                for h in range(NH):
                    reach(pe, "tap0", b, h + 1)
                    project(ZB[h], b, WZ + h * P)

            def sums_as_rows(b, h):
                if h == 0:
                    reach(pe, "scb_r", b, 1)
                    reach(pe, "tap0", b, NC)
                for c in range(NT):
                    col = scb[:, 0, NH * c + h:NH * c + h + 1]
                    mm = pe.matmul(CB[h][:, c * P:(c + 1) * P], col.to_broadcast([P, P]), ident,
                                   start=True, stop=True)
                mm.then_inc(done["csb"], 1)

            def x_by_tokens(b, h):
                reach(pe, "xs_r", b, h + 2)
                if h == 1:
                    reach(pe, "dd_r", b, 4)
                for c in range(NT):
                    mm = pe.transpose(TB[h][:, c * P:(c + 1) * P], xs[:, h, c * P:(c + 1) * P], ident)
                mm.then_inc(done["xtT"], 1)

            def scores(b, h):
                i = h % 2
                reach(pe, "prob", b, h - 1)
                pe.matmul(F[i][0:S, :], kst[:, h, :], qst[:, h // J, :], start=True, stop=False)
                pe.matmul(F[i][0:S, :], sel[:, h:h + 1].to_broadcast([P, S]), mt[:, :],
                          start=False, stop=True).then_inc(done["ksc"], 1)

            def values(b, g):
                reach(pe, "prob", b, J * g + J)
                if g == 0:
                    reach(pe, "copies", b, 8)
                for j in range(J):
                    mm = pe.matmul(F[3][32 * j:32 * j + 32, :], ones[:, 32 * g:32 * g + 32], pr[:, g % 2, j, :],
                                   start=(g == 0), stop=(g == G - 1))
                if g == G - 1:
                    mm.then_inc(done["psum"], 1)
                for j in range(J):
                    mm = pe.matmul(F[2][32 * j:32 * j + 32, :], vst[:, J * g + j, :], pr[:, g % 2, j, :],
                                   start=(g == 0), stop=(g == G - 1))
                mm.then_inc(done["pv"], 1)

            def second_half(m, b):
                if b is not None:
                    project_x(b)
                for h in range(HA // 2, HA):
                    scores(m, h)
                    g, j = divmod(h, J)
                    if j == J - 1:
                        values(m, g - 1)
                    if h == HA - 1 and b is not None:
                        sums_as_rows(b, 0)
                values(m, G - 1)
                if b is not None:
                    sums_as_rows(b, 1)
                    project_z(b)

            def front(b, m):
                if m is not None:
                    second_half(m, b)
                else:
                    project_x(b)
                    steps()
                    pe.wait_ge(su["zero"], 5)
                    pe.wait_ge(su["sel"], 1)
                    pe.wait_ge(su["dt_x"], 1)
                    project_z(b)
                    sums()
                    for h in range(NH):
                        sums_as_rows(b, h)
                if m is not None:
                    attention_out(m)
                x_by_tokens(b, 0)
                reach(pe, "dd_r", b, 8, alone=True)
                for c in range(NT - 1):
                    mm = pe.transpose(F[1][:, c * NS:(c + 1) * NS], xs[0:NS, 2, c * P:(c + 1) * P], ident[0:NS, 0:NS])
                mm.then_inc(done["btT"], 1)
                pe.wait_ge(c_low, 16 * (b + 1))
                for c in range(NT):
                    mm = pe.matmul(F[2][:, c * P:(c + 1) * P], xs[0:NS, 2, c * P:(c + 1) * P],
                                   clow[:, c * P:(c + 1) * P], start=True, stop=True)
                mm.then_inc(done["gdot"], 1)
                x_by_tokens(b, 1)
                if m is not None:
                    columns(m)
                reach(pe, "bw_r", b, 6)
                reach(pe, "xtok_r", b, 2)
                for h in range(NH):
                    for c in range(NT - 1):
                        mm = pe.matmul(F[(1, 3)[h]][0:NS, c * P:(c + 1) * P], bw[:, h, c, :],
                                       xtok(h, c), start=True, stop=True)
                    mm.then_inc(done["upd"], 1)
                reach(pe, "gz_r", b, NH)
                if m is not None:
                    logits(m)
                    unit(m, 0)
                units(m, AT_COLUMNS[1:])
                for h in range(NH):
                    reach(pe, "m_r", b, h + 1)
                    reach(pe, "csd_r", b, h + 1)
                    for c in range(NT):
                        o = F[(0, 2)[h]][:, c * P:(c + 1) * P]
                        mm = pe.matmul(o, xtok(h, c), dd[:, h, c * P:(c + 1) * P],
                                       start=True, stop=(c == 0))
                        if c:
                            reach(pe, "s_r", b, NH * c if c < NT - 1 else 6)
                            mm = pe.matmul(o, st[:, h, c - 1, :], ecs[:, h, c * P:(c + 1) * P],
                                           start=False, stop=True)
                    mm.then_inc(done["ydot"], 1)
                if m is None:
                    keys()
                units(m, AT_GATE)
                if m is None:
                    pe.wait_ge(ld_late, 80)
                reach(pe, "yg_r", b, 2)
                for t in range(NT):
                    for h in range(NH):
                        mm = pe.matmul(F[1][:, t * D:(t + 1) * D], y1[:, h, t * P:(t + 1) * P],
                                       wout[:, h, :], start=(h == 0), stop=(h == NH - 1))
                mm.then_inc(done["wout_d"], 1)
                if m is None:
                    values_in()
                units(m, AT_NORM)
                reach(pe, "norm0", b, 4)
                for t in range(NT):
                    mm = pe.transpose(F[3][:, t * P:(t + 1) * P], x1[:, t, :], ident)
                mm.then_inc(done["x1T"], 1)
                units(m, AT_QUERY[0:1])
                reach(pe, "x1h", b, 1)
                reach(pe, "x1l", b, 1)
                for g in range(G):
                    split3(F[g][:, :], wqH[:, g * P:(g + 1) * P], wqL[:, g * P:(g + 1) * P],
                           x1H[:, :], x1L[:, :], done["qdot"])
                units(m, AT_QUERY[1:])
                reach(pe, "copies", b, 4)
                for i in range(NT * G):
                    t, g = divmod(i, G)
                    if i in (8, 12):
                        units(m, AT_MAX[i // 4 - 2:i // 4 - 1])
                    if t == 0:
                        reach(pe, "qst_r", b, g + 1)
                    else:
                        reach(pe, "tmax", b, i - 3)
                    pe.matmul(F[g][:, 0:J * S], qst[:, g, t * P:(t + 1) * P],
                              kst[:, J * g:J * g + J, :].rearrange("p j s -> p (j s)"),
                              start=True, stop=True).then_inc(done["tsc"], 1)
                units(m, AT_SPLIT)
                reach(pe, "msplit", b, 3)
                for t in range(NT):
                    mm = pe.transpose(F[0][0:2 * HA, t * P:(t + 1) * P],
                                      smHL[:, t, :, :].rearrange("p k h -> p (k h)"), ident)
                mm.then_inc(done["mT"], 1)
                units(m, AT_ROWS)
                reach(pe, "mt_r", b, 1)
                for h in range(HA // 2):
                    scores(b, h)
                    units(m, at_score(h))
                values(b, 0)
                if m is not None:
                    experts_end(m)

            pe.wait_ge(ld_w, 16)
            pe.wait_ge(su["high"], 3)
            pe.wait_ge(su["low"], 3)
            front(0, None)
            pe.wait_ge(su["high"], 7)
            pe.wait_ge(su["low"], 7)
            pe.wait_ge(su["val_in"], 1)
            pe.wait_ge(su["moeH"], 2)
            pe.wait_ge(su["moeL"], 1)
            pe.wait_ge(su["moeLv"], 1)
            pe.wait_ge(ld_moe, 48)
            with pe.Fori(1, NB) as b:
                front(b, b - 1)
            second_half(NB - 1, None)
            attention_out(NB - 1)
            columns(NB - 1)
            unit(NB - 1, 0)
            logits(NB - 1)
            for u in range(1, U):
                unit(NB - 1, u)
            experts_end(NB - 1)

        @block.scalar
        def _(act):
            def setup():
                act.wait_ge(ld_w, 16)
                act.activation(winH[:, WZ:WX], win[:, WZ:WX], ACT.Copy, scale=0.5).then_inc(su["high"], 1)
                act.activation(winH[:, WX:WDT], win[:, WX:WDT], ACT.Copy).then_inc(su["high"], 1)
                act.wait_ge(ld_x0, 16)
                act.activation(xfH[:, 0:L], xf[:, 0:L], ACT.Copy).then_inc(su["high"], 1)
                act.wait_ge(su["taps"], 1)

            def high_parts():
                act.wait_ge(ld_c, 32)
                act.activation(aexp[:, :], sm[:, ALOG:ALOG + NH], ACT.Exp).then_inc(su["aexp"], 1)
                act.wait_ge(ld_ctx, 64)
                act.activation(cxH, cx, ACT.Copy).then_inc(su["high"], 1)
                act.activation(wkH, wqk[:, 1, :], ACT.Copy).then_inc(su["high"], 1)
                act.activation(wqH[:, :], wqk[:, 0, :], ACT.Copy).then_inc(su["high"], 1)
                act.wait_ge(su["dt_neg"], 1)
                act.activation(dtx[:, 1, :], dtx[:, 1, :], ACT.Exp).then_inc(su["dt_exp"], 1)
                act.wait_ge(ld_x, 16)
                act.activation(xfH[:, L:], xf[:, L:], ACT.Copy).then_inc(su["high"], 1)
                act.wait_ge(su["dt_p"], 1)

            def sums():
                act.wait_ge(su["end_d"], 1)
                act.activation(sc[:, :, 2, :], sc[:, :, 2, :], ACT.Exp).then_inc(su["end_exp"], 1)
                act.wait_ge(su["end_p"], 1)
                act.activation(sc[:, :, 3, :], F[2][:, 0:NB * NT * NH].rearrange("p (b c) -> p b c", b=NB),
                               ACT.Exp).then_inc(su["total"], 1)
                act.wait_ge(su["low"], 6)

            def keys():
                for g in range(G):
                    act.wait_ge(su["key_p"], g + 1)
                    act.activation(k32[:, g, :], KB[g][:, 0:NB * S], ACT.Identity,
                                   bias=sm[:, BK + g:BK + g + 1]).then_inc(su["key32"], 1)

            def setup_experts():
                act.wait_ge(ld_moe, 48)
                act.activation(w1H[:, 0, :], w1s[:, 0, :], ACT.Copy, scale=0.5).then_inc(su["moeH"], 1)
                act.activation(w1H[:, 1, :], w1s[:, 1, :], ACT.Copy).then_inc(su["moeH"], 1)
                act.activation(w1s[:, 0, :], w1s[:, 0, :], ACT.Copy, scale=0.5).then_inc(su["moeH"], 1)

            def expert_out(m, e):
                reach(act, "w2d", m, FC * e + FC)
                reach(act, "yadd", m, e - 1)
                if e == 0:
                    reach(act, "lgv", m, 13)
                for t in range(NT):
                    i = act.mul(ye[:, e % 2, t * D:(t + 1) * D], Y[:, t * D:(t + 1) * D], lg[:, 5, t, e:e + 1])
                i.then_inc(done["ye_r"], 1)

            def unit(m, u):
                reach(act, "ab", m, 2 * u + 1)
                reach(act, "moe_h", m, u - 1)
                act.activation(mt_u[:, u % 2, :], M[2 * u % 3][:, :], ACT.Tanh).then_inc(done["tanh_m"], 1)
                if u >= 3 and u % 2 == 1:
                    expert_out(m, u // 2 - 1)

            def units(m, which):
                if m is not None:
                    for u in which:
                        unit(m, u)

            def experts_end(m):
                expert_out(m, E - 1)

            def columns(m):
                reach(act, "x2T", m, 1)
                act.activation(x2H[:, :], F[0][:, :], ACT.Copy).then_inc(done["x2h"], 1)
                act.copy(x2c[:, :], F[0][:, :]).then_inc(done["x2c_r"], 1)

            def router(m):
                reach(act, "lgv", m, 2)
                act.activation(lg[:, 1, :, :], lg[:, 0, :, :], ACT.Exp).then_inc(done["lexp"], 1)

            def taps_in(b, i):
                reach(act, "proj", b, i + 1)
                reach(act, "conv", b - 1, NC * (TAPS - 1))
                act.activation(raw[:, i, TAPS - 1:], XB[i][:, :], ACT.Copy).then_inc(done["raw_c"], 1)
                reach(act, "xs_r", b - 1, 3)
                act.activation(acc[:, i, :], XB[i][:, :], ACT.Identity,
                               bias=cwh[:, NC * TAPS + i:NC * TAPS + i + 1],
                               scale=cwh[:, TAPS * i + 3:TAPS * i + 4]).then_inc(done["tap0"], 1)

            def probability(b, h):
                g, j = divmod(h, J)
                reach(act, "ksc", b, h + 1)
                if g >= 2 and j == 0:
                    reach(act, "pv", b, g - 1)
                act.activation(pr[0:S, g % 2, j, :], F[h % 2][0:S, :], ACT.Exp, scale=SCALE).then_inc(done["prob"], 1)

            def second_half(m, b):
                for h in range(HA // 2, HA):
                    k = h - HA // 2
                    if b is not None and k % 2 == 0 and k < 2 * NC:
                        taps_in(b, k // 2)
                    probability(m, h)

            def front(b, m):
                def decays(h):
                    reach(act, "scb_r", b, 1)
                    reach(act, "csb", b, h + 1)
                    reach(act, "csd_r", b - 1, 2)
                    reach(act, "pv", b - 1, 3)
                    act.activation(ecs[:, h, :], CB[h][0:NS, :], ACT.Exp).then_inc(done["ecs_r"], 1)
                    for c in range(NT):
                        act.activation(dd[:, h, c * P:(c + 1) * P], CB[h][:, c * P:(c + 1) * P], ACT.Relu,
                                       bias=scb[:, 0, NH * c + h:NH * c + h + 1], scale=-1.0).then_inc(done["dd_r"], 1)
                    reach(act, "dd_r", b, NT * (h + 1))
                    act.activation(dd[:, h, :], dd[:, h, :], ACT.Exp, scale=-1.0).then_inc(done["dec"], 1)

                def gate():
                    for h in range(NH):
                        reach(act, "proj", b, 4 + h)
                        reach(act, "gz_r", b - 1, 2)
                        act.activation(gz[:, h, :], ZB[h][:, :], ACT.Tanh).then_inc(done["tanh_z"], 1)

                def silu_x(k):
                    i = LAST_TAP[k]
                    reach(act, "conv", b, NC * (TAPS - 2) + k + 1)
                    act.activation(xs[:, i, :], acc[:, i, :], ACT.Tanh).then_inc(done["tanh_c"], 1)

                if m is None:
                    for i in range(NC):
                        taps_in(b, i)
                    high_parts()
                    gate()
                    for k in range(NC):
                        silu_x(k)
                    sums()
                    for h in range(NH):
                        decays(h)
                else:
                    second_half(m, b)
                    silu_x(0)
                    decays(0)
                    decays(1)
                    silu_x(1)
                    silu_x(2)
                    gate()

                def x_by_tokens(h):
                    reach(act, "xtT", b, h + 1)
                    for c in range(NT):
                        i = act.mul(xtok(h, c), TB[h][:, c * P:(c + 1) * P],
                                    scb[:, 1, NH * c + h:NH * c + h + 1])
                    i.then_inc(done["xtok_r"], 1)

                x_by_tokens(0)
                reach(act, "btT", b, 1)
                for h in range(NH):
                    for c in range(NT - 1):
                        act.mul(bw[:, h, c, :], F[1][:, c * NS:(c + 1) * NS],
                                scb[:, 2, NH * c + h:NH * c + h + 1]).then_inc(done["bw_r"], 1)
                x_by_tokens(1)
                if m is not None:
                    columns(m)
                    units(m, AT_COLUMNS[0:1])
                    router(m)
                units(m, AT_COLUMNS[1:])
                if m is None:
                    keys()
                    setup_experts()
                units(m, AT_GATE)
                units(m, AT_NORM)
                reach(act, "x1T", b, 1)
                act.activation(x1H[:, :], F[3][:, :], ACT.Copy).then_inc(done["x1h"], 1)
                units(m, AT_QUERY[0:1])
                for g in range(G):
                    reach(act, "qdot", b, g + 1)
                    reach(act, "qst_r", b, g - 1)
                    act.activation(q32[:, g % 2, :], F[g][:, :], ACT.Identity,
                                   bias=sm[:, BQ + g:BQ + g + 1]).then_inc(done["q32_r"], 1)
                    if g % 2 == 0:
                        act.activation(qst[:, g, :], F[g][:, :], ACT.Identity,
                                       bias=sm[:, BQ + g:BQ + g + 1]).then_inc(done["qh_r"], 1)
                units(m, AT_QUERY[1:])
                units(m, AT_MAX)
                units(m, AT_SPLIT)
                reach(act, "mT", b, 1)
                act.activation(mt[0:2 * HA, :], F[0][0:2 * HA, :], ACT.Copy).then_inc(done["mt_r"], 1)
                units(m, AT_ROWS)
                for h in range(HA // 2):
                    probability(b, h)
                    units(m, at_score(h))
                if m is not None:
                    experts_end(m)

            setup()
            front(0, None)
            with act.Fori(1, NB) as b:
                front(b, b - 1)
            second_half(NB - 1, None)
            columns(NB - 1)
            unit(NB - 1, 0)
            router(NB - 1)
            for u in range(1, U):
                unit(NB - 1, u)
            experts_end(NB - 1)

        @block.vector
        def _(dve):
            def f32(ap):
                return ap.bitcast(F32)

            def over(ap, n):
                return ap.unsqueeze(1).broadcast_to([ap.shape[0], n, ap.shape[1]])

            def log1p():
                u, s, z, r = dtx[:, 1, :], dtx[:, 2, :], dtx[:, 3, :], dtx[:, 4, :]
                steps = [0]

                def then(i):
                    i.then_inc(su["log1p"], 1)
                    steps[0] += 1
                    dve.wait_ge(su["log1p"], steps[0])

                dve.wait_ge(su["dt_exp"], 1)
                then(dve.tensor_scalar(z, u, 2.0, None, ALU.add))
                then(dve.reciprocal(z, z))
                then(dve.tensor_tensor(s, u, z, ALU.mult))
                then(dve.tensor_tensor(z, s, s, ALU.mult))
                then(dve.tensor_scalar(r, z, 1.0 / (2 * LOG_TERMS + 1), None, ALU.mult))
                for k in range(LOG_TERMS - 1, 0, -1):
                    then(dve.scalar_tensor_tensor(r, r, 1.0 / (2 * k + 1), z, ALU.add, ALU.mult))
                then(dve.tensor_scalar(r, r, 1.0, 2.0, ALU.add, ALU.mult))
                then(dve.tensor_tensor(u, r, s, ALU.mult))

            def setup():
                dve.wait_ge(su["high"], 2)
                dve.scalar_tensor_tensor(winL[:, WZ:WX], win[:, WZ:WX], 0.5, f32(winH[:, WZ:WX]),
                                         ALU.mult, ALU.subtract).then_inc(su["low"], 1)
                dve.tensor_tensor(winL[:, WX:WDT], win[:, WX:WDT], f32(winH[:, WX:WDT]), ALU.subtract).then_inc(su["low"], 1)
                dve.wait_ge(su["high"], 3)
                dve.tensor_tensor(xfL[:, 0:L], xf[:, 0:L], f32(xfH[:, 0:L]), ALU.subtract).then_inc(su["low"], 1)
                dve.wait_ge(ld_c, 32)
                dve.tensor_scalar(cwh[:, :], sm[:, CW:CW + NC * TAPS + NC], 0.5, None, ALU.mult).then_inc(su["taps"], 1)
                dve.wait_ge(su["zero"], 1)

            def steps():
                dve.wait_ge(su["dt_p"], 1)
                dve.tensor_tensor(dtx[:, 0, :].rearrange("p (t h) -> p t h", h=NH),
                                  F[0][:, 0:NB * NT * NH].rearrange("p (t h) -> p t h", h=NH),
                                  over(sm[:, DTB:DTB + NH], NB * NT), ALU.add).then_inc(su["dt_x"], 1)
                dve.wait_ge(su["dt_x"], 1)
                dve.scalar_tensor_tensor(dtx[:, 1, :], dtx[:, 0, :], -1.0, dtx[:, 0, :], ALU.mult, ALU.min).then_inc(su["dt_neg"], 1)

            def step_sizes():
                log1p()
                dve.scalar_tensor_tensor(sc[:, :, 1, :], dtx[:, 0, :].rearrange("p (b c) -> p b c", b=NB), 0.0,
                                         dtx[:, 1, :].rearrange("p (b c) -> p b c", b=NB),
                                         ALU.max, ALU.add).then_inc(su["dt"], 1)
                dve.wait_ge(su["dt"], 1)
                dve.wait_ge(su["aexp"], 1)
                for b in range(NB):
                    i = dve.scalar_tensor_tensor(
                        dta[:, b * NT * NH:(b + 1) * NT * NH].rearrange("p (t h) -> p t h", h=NH),
                        sc[:, b, 1, :].rearrange("p (t h) -> p t h", h=NH), -1.0, over(aexp[:, :], NT),
                        ALU.mult, ALU.mult)
                i.then_inc(su["dta"], 1)
                dve.wait_ge(su["dta"], 1)
                dve.tensor_scalar(dta[:, :], dta[:, :], UNDERFLOW, None, ALU.max).then_inc(su["dta"], 1)
                dve.wait_ge(su["high"], 6)
                dve.tensor_tensor(cxL, cx, f32(cxH), ALU.subtract).then_inc(su["low"], 1)
                dve.tensor_tensor(wkL, wqk[:, 1, :], f32(wkH), ALU.subtract).then_inc(su["low"], 1)
                dve.tensor_tensor(wqL[:, :], wqk[:, 0, :], f32(wqH[:, :]), ALU.subtract).then_inc(su["low"], 1)
                dve.wait_ge(su["high"], 7)
                dve.tensor_tensor(xfL[:, L:], xf[:, L:], f32(xfH[:, L:]), ALU.subtract).then_inc(su["low"], 1)

            def sums():
                dve.wait_ge(su["cs_p"], 1)
                dve.tensor_copy(sc[:, :, 0, :], F[1][:, 0:NB * NT * NH].rearrange("p (b c) -> p b c", b=NB)).then_inc(su["cs"], 1)
                dve.wait_ge(su["cs"], 1)
                dve.wait_ge(su["end_p"], 1)
                dve.tensor_tensor(sc[:, :, 2, :], F[2][:, 0:NB * NT * NH].rearrange("p (b c) -> p b c", b=NB),
                                  sc[:, :, 0, :], ALU.subtract).then_inc(su["end_d"], 1)

            def keys(g):
                dve.wait_ge(su["key32"], g + 1)
                if g:
                    dve.wait_ge(su["key_in"], g)
                dve.tensor_copy(kH, k32[:, g, :]).then_inc(su["keyH"], 1)
                dve.wait_ge(su["keyH"], g + 1)
                dve.scalar_tensor_tensor(kst0, f32(kH), con[:, MK:MK + 1], k32[:, g, :],
                                         ALU.mult, ALU.add).then_inc(su["keyS"], 1)
                dve.wait_ge(su["keyS"], g + 1)
                dve.tensor_scalar(kc[:, :, g, :], kst0.rearrange("p (b s) -> p b s", b=NB),
                                  con[:, KEEP:KEEP + 1], None, ALU.mult).then_inc(su["key_in"], 1)

            def values_in():
                dve.wait_ge(su["val_p"], 1)
                dve.wait_ge(ld_late, 80)
                dve.tensor_tensor(vc[:, :, :], M[0][0:S, :].rearrange("p (b d) -> p b d", b=NB), over(bv[:, :], NB),
                                  ALU.add).then_inc(su["val_in"], 1)

            def unit(m, u):
                a, k = M[2 * u % 3], M[(2 * u + 1) % 3]
                reach(dve, "tanh_m", m, u + 1)
                dve.scalar_tensor_tensor(mt_u[:, u % 2, :], mt_u[:, u % 2, :], 1.0, a[:, :],
                                         ALU.add, ALU.mult).then_inc(done["moe_u"], 1)
                reach(dve, "moe_u", m, u + 1)
                reach(dve, "ab", m, 2 * u + 2)
                reach(dve, "w2d", m, u - 2)
                dve.tensor_tensor(mt_h[:, u % 3, :], mt_u[:, u % 2, :], k[:, :], ALU.mult).then_inc(done["moe_h"], 1)

            def units(m, which):
                if m is not None:
                    for u in which:
                        unit(m, u)

            def statistics(k, b):
                if k == 2:
                    reach(dve, "yadd", b, E)
                else:
                    reach(dve, f"res{k}", b, 1)
                for t in range(NT):
                    dve.bn_stats(bst[:, k, t, :], res[k][:, t, :]).then_inc(done[f"stat{k}"], 1)
                for t in range(NT):
                    reach(dve, f"stat{k}", b, t + 1, alone=True)
                    dve.bn_aggr(mv[:, k, t, :], bst[:, k, t, :]).then_inc(done[f"mv{k}"], 1)

            def normalise(k, b, out):
                reach(dve, f"mv{k}", b, NT)
                reach(dve, f"rstd{k}", b, 1)
                for t in range(NT):
                    dve.tensor_scalar(out[:, t, :], res[k][:, t, :], mv[:, k, t, 0:1], rstd[:, k, 1, t:t + 1],
                                      ALU.subtract, ALU.mult).then_inc(done[f"norm{k}"], 1)

            def front(b, m):
                def tap_one(i, k):
                    dve.scalar_tensor_tensor(acc[:, i, :], raw[:, i, k:k + L], cwh[:, TAPS * i + k:TAPS * i + k + 1],
                                             acc[:, i, :], ALU.mult, ALU.add).then_inc(done["conv"], 1)

                def gate():
                    for h in range(NH):
                        reach(dve, "tanh_z", b, h + 1)
                        dve.scalar_tensor_tensor(gz[:, h, :], gz[:, h, :], 1.0, ZB[h][:, :],
                                                 ALU.add, ALU.mult).then_inc(done["gz_r"], 1)

                def silu_x(k):
                    i = LAST_TAP[k]
                    reach(dve, "tanh_c", b, k + 1)
                    dve.scalar_tensor_tensor(xs[:, i, :], xs[:, i, :], 1.0, acc[:, i, :],
                                             ALU.add, ALU.mult).then_inc(done["xs_r"], 1)

                for i in range(NC):
                    reach(dve, "tap0", b, i + 1)
                    tap_one(i, 2)
                for i in range(NC):
                    reach(dve, "conv", b, i + 1)
                    tap_one(i, 1)
                if m is None:
                    steps()
                for k, i in enumerate(LAST_TAP):
                    reach(dve, "conv", b, NC + i + 1)
                    tap_one(i, 0)
                if m is None:
                    step_sizes()
                    gate()
                    sums()
                    for k in range(NC):
                        silu_x(k)
                else:
                    dve.wait_ge(c_low, 16 * b)
                    silu_x(0)
                    divide(m)
                    silu_x(1)
                    add_attention(m)
                    silu_x(2)
                    normalise(1, m, res[1])
                    gate()
                reach(dve, "gdot", b, 1)
                for h in range(NH):
                    reach(dve, "mask_r", b, h + 1)
                    dve.tensor_tensor(dd[:, h, :], dd[:, h, :], F[2][:, :], ALU.mult).then_inc(done["m_r"], 1)
                if m is not None:
                    low_columns(m)
                for c in range(NT - 1):
                    for h in range(NH):
                        new = F[(1, 3)[h]][0:NS, c * P:(c + 1) * P]
                        if c == 0:
                            reach(dve, "upd", b, h + 1)
                            i = dve.tensor_copy(st[:, h, 0, :], new)
                        else:
                            reach(dve, "s_r", b, NH * (c - 1) + h + 1)
                            i = dve.scalar_tensor_tensor(st[:, h, c, :], st[:, h, c - 1, :],
                                                         scb[0:NS, 3, NH * c + h:NH * c + h + 1], new,
                                                         ALU.mult, ALU.add)
                        i.then_inc(done["s_r"], 1)
                if m is not None:
                    router_logits(m)
                    unit(m, 0)
                units(m, AT_COLUMNS[1:])
                if m is not None:
                    router(m)
                for h in range(NH):
                    reach(dve, "ydot", b, h + 1)
                    dve.scalar_tensor_tensor(y1[:, h, :], xs[:, h, :], sm[:, DSK + h:DSK + h + 1],
                                             F[(0, 2)[h]][:, :], ALU.mult, ALU.add).then_inc(done["y1_r"], 1)
                    reach(dve, "y1_r", b, h + 1)
                    dve.tensor_tensor(y1[:, h, :], y1[:, h, :], gz[:, h, :], ALU.mult).then_inc(done["yg_r"], 1)
                units(m, AT_GATE)
                if m is not None:
                    router_weights(m)
                if m is None:
                    keys(0)
                reach(dve, "wout_d", b, 1)
                dve.wait_ge(ld_tok, 16 * (b + 1))
                dve.tensor_tensor(res[0][:, :, :], F[1][:, :].rearrange("p (t d) -> p t d", t=NT),
                                  xt[:, :, :], ALU.add).then_inc(done["res0"], 1)
                statistics(0, b)
                units(m, AT_NORM[0:1])
                if m is None:
                    keys(1)
                normalise(0, b, x1)
                if m is None:
                    keys(2)
                    values_in()
                units(m, AT_NORM[1:])
                reach(dve, "x1h", b, 1)
                dve.tensor_tensor(x1L[:, :], F[3][:, :], f32(x1H[:, :]), ALU.subtract).then_inc(done["x1l"], 1)
                if m is None:
                    keys(3)
                units(m, AT_QUERY[0:1])
                for g in range(G):
                    if g % 2 == 0:
                        reach(dve, "qh_r", b, g // 2 + 1)
                    else:
                        reach(dve, "q32_r", b, g + 1)
                        dve.tensor_copy(qst[:, g, :], q32[:, g % 2, :]).then_inc(done["qc_r"], 1)
                        reach(dve, "qc_r", b, g // 2 + 1)
                    dve.scalar_tensor_tensor(qst[:, g, :], f32(qst[:, g, :]), con[:, MQ:MQ + 1], q32[:, g % 2, :],
                                             ALU.mult, ALU.add).then_inc(done["qst_r"], 1)
                for i in range(NT * G):
                    t, g = divmod(i, G)
                    if i == 4:
                        units(m, AT_QUERY[1:])
                    if i in (8, 12):
                        units(m, AT_MAX[i // 4 - 2:i // 4 - 1])
                    reach(dve, "tsc", b, i + 1)
                    dve.tensor_reduce(smax[:, t, J * g:J * g + J], F[g][:, 0:J * S].rearrange("p (j s) -> p j s", j=J),
                                      AX.X, ALU.max).then_inc(done["tmax"], 1)
                reach(dve, "tmax", b, NT * G)
                dve.tensor_copy(smH[:, :, :], smax[:, :, :]).then_inc(done["msplit"], 1)
                reach(dve, "msplit", b, 1)
                dve.tensor_copy(smHL[:, :, 0, :], f32(smH[:, :, :])).then_inc(done["msplit"], 1)
                dve.tensor_tensor(smHL[:, :, 1, :], smax[:, :, :], f32(smH[:, :, :]), ALU.subtract).then_inc(done["msplit"], 1)
                units(m, AT_SPLIT)
                units(m, AT_ROWS)
                units(m, AT_SCORE)
                if m is None:
                    dve.wait_ge(su["moeH"], 3)
                    dve.tensor_tensor(w1L[:, 0, :], w1s[:, 0, :], f32(w1H[:, 0, :]), ALU.subtract).then_inc(su["moeL"], 1)
                if m is not None:
                    statistics(2, m)
                    normalise(2, m, res[2])

            def divide(b):
                reach(dve, "psum", b, 1)
                for k in range(2):
                    half_row = slice(k * L // 2, (k + 1) * L // 2)
                    dve.reciprocal(rsum[:, half_row], F[3][:, half_row]).then_inc(done["rs_r"], 1)
                    reach(dve, "rs_r", b, k + 1)
                    reach(dve, "pv", b, G)
                    dve.tensor_tensor(att[:, half_row], F[2][:, half_row], rsum[:, half_row], ALU.mult).then_inc(done["att_r"], 1)

            def add_attention(b):
                reach(dve, "wo_d", b, 1)
                reach(dve, "bo_r", b, 1)
                dve.tensor_tensor(res[1][:, :, :], F[0][:, :].rearrange("p (t d) -> p t d", t=NT),
                                  x1bo[:, :, :], ALU.add).then_inc(done["res1"], 1)
                statistics(1, b)

            def low_columns(b):
                reach(dve, "x2h", b, 1)
                reach(dve, "x2c_r", b, 1)
                dve.tensor_tensor(x2L[:, :], F[0][:, :], f32(x2H[:, :]), ALU.subtract).then_inc(done["x2l"], 1)

            def per_expert(ap):
                return ap.unsqueeze(2).broadcast_to([P, NT, E])

            def router_logits(b):
                logits = Y[:, 0:NT * E].rearrange("p (t e) -> p t e", t=NT)
                reach(dve, "logit", b, 1)
                dve.tensor_reduce(lmx[:, 0, :], logits, AX.X, ALU.max).then_inc(done["lgv"], 1)
                reach(dve, "lgv", b, 1)
                dve.tensor_tensor(lg[:, 0, :, :], logits, per_expert(lmx[:, 0, :]), ALU.subtract).then_inc(done["lgv"], 1)

            def after_logits(b, step):
                def then(i, alone=False):
                    nonlocal step
                    i.then_inc(done["lgv"], 1)
                    step += 1
                    reach(dve, "lgv", b, step, alone)
                return then

            def router(b):
                then = after_logits(b, 2)

                reach(dve, "lexp", b, 1)
                then(dve.tensor_reduce(lmx[:, 1, :], lg[:, 1, :, :], AX.X, ALU.add))
                then(dve.reciprocal(lmx[:, 2, :], lmx[:, 1, :]))
                then(dve.tensor_tensor(lg[:, 2, :, :], lg[:, 1, :, :], per_expert(lmx[:, 2, :]), ALU.mult), alone=True)
                for t in range(NT):
                    dve.max(top[:, t, :], lg[:, 2, t, :]).then_inc(done["topv"], 1)
                for t in range(NT):
                    reach(dve, "topv", b, t + 1, alone=True)
                    dve.max_index(topi[:, t, :], top[:, t, :], lg[:, 2, t, :]).then_inc(done["topv"], 1)

            def router_weights(b):
                then = after_logits(b, 5)
                reach(dve, "topv", b, 2 * NT)
                then(dve.tensor_copy(topf[:, :, :], topi[:, :, :]))
                then(dve.tensor_tensor(lmx[:, 1, :], top[:, :, 0], top[:, :, 1], ALU.add))
                then(dve.reciprocal(lmx[:, 3, :], lmx[:, 1, :]))
                iota = con[:, IOTA:IOTA + E]
                iotas = over(iota, NT)
                then(dve.tensor_tensor(lg[:, 3, :, :], iotas, per_expert(topf[:, :, 0]), ALU.is_equal))
                then(dve.tensor_tensor(lg[:, 4, :, :], iotas, per_expert(topf[:, :, 1]), ALU.is_equal))
                then(dve.tensor_tensor(lg[:, 3, :, :], lg[:, 3, :, :], lg[:, 4, :, :], ALU.add))
                then(dve.tensor_tensor(lg[:, 4, :, :], lg[:, 2, :, :], lg[:, 3, :, :], ALU.mult))
                then(dve.tensor_tensor(lg[:, 5, :, :], lg[:, 4, :, :], per_expert(lmx[:, 3, :]), ALU.mult))

            setup()
            front(0, None)
            with dve.Fori(1, NB) as b:
                front(b, b - 1)
            divide(NB - 1)
            add_attention(NB - 1)
            normalise(1, NB - 1, res[1])
            low_columns(NB - 1)
            unit(NB - 1, 0)
            router_logits(NB - 1)
            router(NB - 1)
            unit(NB - 1, 1)
            router_weights(NB - 1)
            for u in range(2, U):
                unit(NB - 1, u)
            statistics(2, NB - 1)
            normalise(2, NB - 1, res[2])

        @block.gpsimd
        def _(pool):
            def setup():
                pool.memset(half[:, :], -0.5).then_inc(su["half"], 1)
                pool.wait_ge(su["half"], 1)
                pool.memset(raw[:, :, 0:TAPS - 1], 0.0).then_inc(su["zero"], 1)
                pool.memset(kst[:, :, :].bitcast(F32), 0.0).then_inc(su["zero"], 1)
                pool.memset(vst[:, :, :], 0.0).then_inc(su["zero"], 1)
                pool.memset(mt[:, :].bitcast(F32), 0.0).then_inc(su["zero"], 1)
                pool.wait_ge(su["zero"], 4)
                pool.memset(pr[64:P, :, :, :], 0.0).then_inc(su["zero"], 1)
                pool.wait_ge(su["zero"], 5)
                pool.wait_ge(ld_c, 32)
                pool.tensor_copy(sel[:, :], con[:, IND:IND + HA + E]).then_inc(su["sel"], 1)

            def setup_experts():
                pool.wait_ge(su["moeH"], 2)
                pool.tensor_tensor(w1L[:, 1, :], w1s[:, 1, :], w1H[:, 1, :].bitcast(F32), ALU.subtract).then_inc(su["moeLv"], 1)

            def static_copies(b):
                if isinstance(b, int):
                    pool.wait_ge(su["key_in"], G)
                    pool.wait_ge(su["val_in"], 1)
                    pool.wait_ge(su["zero"], 3)
                    pool.wait_ge(done["rstd0"], 1)
                else:
                    reach(pool, "pv", b - 1, G)
                    reach(pool, "scb_r", b, 1)
                for j in range(J):
                    reach(pool, "copies", b, j)
                    rows = slice(32 * j, 32 * j + 32)
                    pool.tensor_copy(kst[rows, j:HA:J, :], kc[rows, b, :, :]).then_inc(done["copies"], 1)
                reach(pool, "copies", b, J)
                for g in range(G):
                    pool.tensor_copy(vst[0:S, J * g:J * g + J, DH * g:DH * g + DH],
                                     vc[:, b, 32 * g:32 * g + 32].rearrange("p (j d) -> p j d", j=J)).then_inc(done["copies"], 1)

            def expert_add(m, e):
                reach(pool, "yadd", m, e)
                reach(pool, "ye_r", m, e + 1)
                if e == 0 and isinstance(m, int):
                    pool.wait_ge(stored, 16 * m)
                elif e == 0:
                    pool.wait_ge(ld_tok, 16 * (m + 2))
                pool.tensor_tensor(res[2][:, :, :], ye[:, e % 2, :].rearrange("p (t d) -> p t d", t=NT),
                                   res[1 if e == 0 else 2][:, :, :], ALU.add).then_inc(done["yadd"], 1)

            def unit(m, u):
                if u >= 4 and u % 2 == 0:
                    expert_add(m, u // 2 - 2)

            def experts_end(m):
                expert_add(m, E - 2)
                expert_add(m, E - 1)
                deviation(2, m)

            def units(m, which):
                if m is not None:
                    for u in which:
                        unit(m, u)

            def deviation(k, b):
                reach(pool, f"mv{k}", b, NT, alone=True)
                pool.tensor_scalar(rstd[:, k, 0, :], mv[:, k, :, 1], EPS, None, ALU.add).then_inc(done[f"eps{k}"], 1)
                reach(pool, f"eps{k}", b, 1)
                pool.tensor_tensor(rstd[:, k, 1, :], rstd[:, k, 0, :], half[:, :], ALU.pow).then_inc(done[f"rstd{k}"], 1)

            def front(b, m):
                if m is None:
                    pool.wait_ge(su["end_exp"], 1)
                    pool.wait_ge(su["total"], 1)
                    pool.wait_ge(ld_late, 80)
                pool.tensor_copy(scb[:, :, :], sc[:, b, :, :]).then_inc(done["scb_r"], 1)
                for h in range(NH):
                    reach(pool, "dec", b, h + 1)
                    dd_h = dd[:, h, :].rearrange("p (c q) -> p c q", c=NT)
                    pool.tensor_tensor(dd_h, dd_h, tri.unsqueeze(1).broadcast_to([P, NT, P]), ALU.mult).then_inc(done["mask_r"], 1)
                    if h == 0 and m is not None:
                        deviation(1, m)
                pool.wait_ge(c_low, 16 * (b + 1))
                for h in range(NH):
                    reach(pool, "ecs_r", b, h + 1)
                    pool.tensor_tensor(ecs[:, h, :], clow[:, :], ecs[:, h, :], ALU.mult).then_inc(done["csd_r"], 1)
                units(m, AT_COLUMNS)
                if m is not None:
                    static_copies(b)
                units(m, AT_GATE)
                deviation(0, b)
                if m is None:
                    static_copies(b)
                units(m, AT_NORM)
                reach(pool, "norm0", b, NT)
                pool.tensor_tensor(x1bo[:, :, :], x1[:, :, :], bo[:, :].unsqueeze(1).broadcast_to([P, NT, D]),
                                   ALU.add).then_inc(done["bo_r"], 1)
                if m is None:
                    setup_experts()
                units(m, AT_QUERY)
                units(m, AT_MAX)
                units(m, AT_SPLIT)
                units(m, AT_ROWS)
                units(m, AT_SCORE)
                if m is not None:
                    experts_end(m)

            setup()
            front(0, None)
            with pool.Fori(1, NB) as b:
                front(b, b - 1)
            deviation(1, NB - 1)
            for u in range(U):
                unit(NB - 1, u)
            experts_end(NB - 1)


def kernel(**inputs):
    import concourse.bacc as bacc
    from concourse.bass_utils import run_bass_kernel_spmd

    a = {k: np.asarray(v) for k, v in inputs.items()}
    heads = np.arange(HA).reshape(G, J)
    stacked = (heads[:, :, None] * DH + (np.arange(32) % DH)[None, None, :]).reshape(-1)
    packed = (heads.T[:, :, None] * DH + np.arange(DH)[None, None, :]).reshape(-1)
    x = a["x"].reshape(NB * L, D)
    small = np.concatenate([
        a["L0_attn_conv_w"].reshape(NC, P, TAPS).transpose(1, 0, 2).reshape(P, NC * TAPS),
        a["L0_attn_conv_b"].reshape(NC, P).T,
        np.broadcast_to(a["L0_attn_A_log"], (P, NH)),
        np.broadcast_to(a["L0_attn_dt_bias"], (P, NH)),
        np.broadcast_to(a["L0_attn_D_skip"], (P, NH)),
        a["L0_xattn_bq"][stacked].reshape(G, P).T,
        a["L0_xattn_bk"][stacked].reshape(G, P).T,
    ], axis=1)
    arrays = {
        "x_feat": x.T,
        "x_tok": x.reshape(NB, NT, P, D).transpose(2, 0, 1, 3),
        "ctx_feat": a["ctx_1024"].reshape(NB * S, D).T,
        "small": small,
        "cst": constants(),
        "bv_row": np.broadcast_to(a["L0_xattn_bv"], (S, D)),
        "bo_row": np.broadcast_to(a["L0_xattn_bo"], (P, D)),
        "w_in": a["L0_attn_W_in"].T,
        "w_out": a["L0_attn_W_out"].T.reshape(NH, P, D).transpose(1, 0, 2),
        "wq": a["L0_xattn_Wq"].T[:, stacked],
        "wk": a["L0_xattn_Wk"].T[:, stacked],
        "wv": a["L0_xattn_Wv"].T,
        "wo": a["L0_xattn_Wo"].T[packed, :],
        "router": a["L0_ffn_router_w"].T,
        "w1": a["L0_ffn_w1"].transpose(2, 0, 1).reshape(D, E * FC * P),
        "v1": a["L0_ffn_v1"].transpose(2, 0, 1).reshape(D, E * FC * P),
        "w2": a["L0_ffn_w2"].reshape(E * FC, P, D).transpose(1, 0, 2),
    }
    arrays = {k: np.ascontiguousarray(v) for k, v in arrays.items()}
    nc = bacc.Bacc("TRN2", target_bir_lowering=False, num_devices=1)
    args = {k: nc.dram_tensor(k, v.shape, mybir.dt.from_np(v.dtype), kind="ExternalInput").ap()
            for k, v in arrays.items()}
    out = nc.dram_tensor("out", (P, NB, NT, D), F32, kind="ExternalOutput").ap()
    decoder_kernel(nc, **args, out=out)
    r = run_bass_kernel_spmd(nc, [arrays], core_ids=[0])
    return r.results[0]["out"].transpose(1, 2, 0, 3).reshape(NB, L, D)
```
